# Optimizing a Trainium2 kernel written in Bass

```python
import numpy as np
import jax
import jax.numpy as jnp

def _softmax(x, axis=-1):
    return jax.nn.softmax(x, axis=axis)

def _gelu(x):
    return jax.nn.gelu(x, approximate=True)

def _silu(x):
    return jax.nn.silu(x)

def _sigmoid(x):
    return jax.nn.sigmoid(x)

def _layernorm(x, axis=-1, eps=1e-05):
    m = jnp.mean(x, axis=axis, keepdims=True)
    v = jnp.var(x, axis=axis, keepdims=True)
    return (x - m) / jnp.sqrt(v + eps)

def _scatter_add(tgt, idx, src, axis=0):
    return tgt.at[idx].add(src)

def _segment_sum(src, seg, n):
    return jax.ops.segment_sum(src, seg, n)
kernel_name = 'mk_flamingo_gated_d1_seqx_r4_7b8cae'

def setup_inputs(seed: int=0):
    np.random.seed(seed)
    _w = jnp.asarray

    def _rec_inputs():
        import jax
        import jax.numpy as jnp
        _rk = jax.random.key(seed)
        x = 7.22e-05 + 1 * jax.random.normal(jax.random.fold_in(_rk, 1), (4, 512, 512), jnp.float32)
        _lenS = 512 - jax.random.randint(jax.random.fold_in(_rk, 7), (4,), 0, max(1, 512 // 4) + 1, jnp.int32)
        _lenS2 = 512 - jax.random.randint(jax.random.fold_in(_rk, 8), (4,), 0, max(1, 512 // 4) + 1, jnp.int32)
        _ctx_1024P = jax.random.normal(jax.random.fold_in(_rk, 11), (4, 16, 256), jnp.float32)
        _ctx_1024c = jax.random.dirichlet(jax.random.fold_in(_rk, 511), 0.3 * jnp.ones((16,), jnp.float32), (4, 512))
        _ctx_1024t = jnp.einsum('bsk,bkd->bsd', _ctx_1024c, _ctx_1024P)
        _ctx_1024t = _ctx_1024t * jax.lax.rsqrt(jnp.mean(jnp.square(_ctx_1024t)) + 1e-12) * 0.953939
        ctx_1024 = 2.81802e-05 + 1.00001 * (_ctx_1024t + 0.3 * jax.random.normal(jax.random.fold_in(_rk, 611), (4, 512, 256), jnp.float32))
        _g = jax.random.normal(jax.random.fold_in(_rk, 9001), (2, 1), jnp.float32)
        _g = jnp.sign(_g) * jnp.maximum(jnp.abs(_g), 1.0) + (_g == 0) * 1.0
        g_xattn = _g[0]
        g_ffn = _g[1]
        return (x, ctx_1024, g_xattn, g_ffn)
    x, ctx_1024, g_xattn, g_ffn = _rec_inputs()

    def _L0_xattn_setup():
        import jax, jax.numpy as jnp
        import numpy as np
        key = jax.random.key(seed)
        ks = jax.random.split(key, 6)
        B, L, N, C, D = (8, 128, 512, 256, 128)
        return {'teacher_logits': jax.random.normal(ks[0], (B, L, N), dtype=jnp.float32), 'teacher_features': jax.random.normal(ks[1], (B, N, C), dtype=jnp.float32), 'Wq': jax.random.normal(ks[2], (D, C), dtype=jnp.float32) * (1.0 / np.sqrt(C)), 'bq': jnp.zeros((D,), dtype=jnp.float32), 'Wk': jax.random.normal(ks[3], (D, C), dtype=jnp.float32) * (1.0 / np.sqrt(C)), 'bk': jnp.zeros((D,), dtype=jnp.float32)}
    _L0_xattn_all = _L0_xattn_setup()
    _L0_xattn_in = {k: v for k, v in _L0_xattn_all.items() if k in ('Wq', 'bq', 'Wk', 'bk')}
    del _L0_xattn_all

    def _L0_ffn_setup():
        import jax, jax.numpy as jnp
        import numpy as np
        D_IN = 512
        D_OUT = 512
        EPS = 1e-05
        key = jax.random.key(seed)
        k_x, k_w = jax.random.split(key)
        x = jax.random.normal(k_x, (8, 512, D_IN), dtype=jnp.float32)
        weight = jax.random.normal(k_w, (D_OUT, D_IN), dtype=jnp.float32)
        gamma = jnp.ones((D_OUT,), dtype=jnp.float32)
        beta = jnp.zeros((D_OUT,), dtype=jnp.float32)
        ln_weight = jnp.ones((D_IN,), dtype=jnp.float32)
        ln_bias = jnp.zeros((D_IN,), dtype=jnp.float32)
        return {'x': x, 'weight': weight, 'gamma': gamma, 'beta': beta, 'ln_weight': ln_weight, 'ln_bias': ln_bias}
    _L0_ffn_all = _L0_ffn_setup()
    _L0_ffn_in = {k: v for k, v in _L0_ffn_all.items() if k in ('weight', 'gamma', 'beta', 'ln_weight', 'ln_bias')}
    del _L0_ffn_all
    return {'x': x, 'ctx_1024': ctx_1024, 'g_xattn': g_xattn, 'g_ffn': g_ffn, 'L0_xattn_Wq': _L0_xattn_in['Wq'], 'L0_xattn_bq': _L0_xattn_in['bq'], 'L0_xattn_Wk': _L0_xattn_in['Wk'], 'L0_xattn_bk': _L0_xattn_in['bk'], 'L0_ffn_weight': _L0_ffn_in['weight'], 'L0_ffn_gamma': _L0_ffn_in['gamma'], 'L0_ffn_beta': _L0_ffn_in['beta'], 'L0_ffn_ln_weight': _L0_ffn_in['ln_weight'], 'L0_ffn_ln_bias': _L0_ffn_in['ln_bias']}

def reference(x, ctx_1024, g_xattn, g_ffn, L0_xattn_Wq, L0_xattn_bq, L0_xattn_Wk, L0_xattn_bk, L0_ffn_weight, L0_ffn_gamma, L0_ffn_beta, L0_ffn_ln_weight, L0_ffn_ln_bias):
    import jax
    import jax.numpy as jnp

    def _L0_xattn_ref(teacher_logits, teacher_features, Wq, bq, Wk, bk):
        import jax, jax.numpy as jnp
        import numpy as np
        query = jnp.einsum('bnc,dc->bnd', teacher_features, Wq) + bq
        key = jnp.einsum('bnc,dc->bnd', teacher_features, Wk) + bk
        energy = jnp.einsum('bnd,bmd->bnm', query, key)
        attention = jax.nn.softmax(energy, axis=-1)
        x_m = jnp.einsum('bln,bmn->blm', teacher_logits, attention)
        return x_m

    def _L0_ffn_ref(x, weight, gamma, beta, ln_weight, ln_bias):
        import jax, jax.numpy as jnp
        import numpy as np
        D_IN = 512
        D_OUT = 512
        EPS = 1e-05
        mean = jnp.mean(x, axis=-1, keepdims=True)
        var = jnp.mean(jnp.square(x - mean), axis=-1, keepdims=True)
        xn = (x - mean) * jax.lax.rsqrt(var + EPS) * ln_weight + ln_bias
        quant_w = jnp.sign(weight)
        scale = jnp.max(jnp.abs(weight))
        out = jnp.einsum('bsk,ok->bso', xn, quant_w)
        return out * scale * gamma + beta
    x = x + jnp.tanh(g_xattn[0]) * _L0_xattn_ref(_layernorm(x, axis=-1), ctx_1024, L0_xattn_Wq, L0_xattn_bq, L0_xattn_Wk, L0_xattn_bk)
    x = x + jnp.tanh(g_ffn[0]) * _L0_ffn_ref(_layernorm(x, axis=-1), L0_ffn_weight, L0_ffn_gamma, L0_ffn_beta, L0_ffn_ln_weight, L0_ffn_ln_bias)
    return x

_drawn_inputs = setup_inputs


def setup_inputs(seed=0):
    import zlib

    import numpy as np

    out = dict(_drawn_inputs(seed))
    spreads = {'L0_xattn_bq': (0.0, 0.1),
     'L0_xattn_bk': (0.0, 0.1),
     'L0_ffn_gamma': (1.0, 0.2),
     'L0_ffn_beta': (0.0, 0.1),
     'L0_ffn_ln_weight': (1.0, 0.2),
     'L0_ffn_ln_bias': (0.0, 0.1)}
    factors = {}
    for name, (base, spread) in spreads.items():
        noise = np.random.default_rng([zlib.crc32(name.encode()), seed]).standard_normal(out[name].shape)
        drawn = base * np.exp(spread * noise) if base else spread * noise
        out[name] = jnp.asarray(drawn.astype(out[name].dtype))
    for name, factor in factors.items():
        out[name] = (out[name] * factor).astype(out[name].dtype)
    return out
```

```python
import concourse.bass as bass
from concourse import mybir
from contextlib import ExitStack


def flamingo_block_kernel(nc, x, x_t, ctx_t, g_xattn, g_ffn, wq_t, bq, wk_t, bk,
                          weight_t, gamma, beta, ln_weight, ln_bias_t, out):
    f32 = mybir.dt.float32
    f32r = mybir.dt.float32r
    ALU = mybir.AluOpType
    ACT = mybir.ActivationFunctionType
    AX = mybir.AxisListType

    P = 128
    B, L, N = x.shape
    C = ctx_t.shape[1]
    D = wq_t.shape[1]
    T = L // P
    KN = N // P
    KC = C // P
    EPS = 1e-5

    SCORE_USES = 2 + T
    TURN_USES = 2 * T

    es = ExitStack()
    with es:
        def sb(name, shape, dt=f32):
            return es.enter_context(nc.sbuf_tensor(name, shape, dt))

        def pb(name, shape):
            return es.enter_context(nc.psum_tensor(name, shape, f32))

        def sem(name):
            return es.enter_context(nc.semaphore(name))

        wq_sb = sb("wq_sb", [P, KC, D])
        wk_sb = sb("wk_sb", [P, KC, D])
        bqk = sb("bqk", [P, 2])
        w_raw = sb("w_raw", [P, KN, N])
        w_sign = sb("w_sign", [P, KN, N], f32r)
        ln_w = sb("ln_w", [P, N])
        gain = sb("gain", [P, N])
        shift = sb("shift", [P, N])
        shift_h = sb("shift_h", [P, N])
        lnb_col = sb("lnb_col", [P, KN])
        lnb_hi = sb("lnb_hi", [P, KN, P], f32r)
        lnb_lo = sb("lnb_lo", [P, KN, P], f32r)
        gates = sb("gates", [P, 2])
        tanh_g = sb("tanh_g", [P, 2])
        w_max = sb("w_max", [P, 1])
        w_scale = sb("w_scale", [P, 1])
        ident = sb("ident", [P, P])
        neg_half = sb("neg_half", [P, T])

        ctx_sb = sb("ctx_sb", [P, KC, L])
        x_sb = sb("x_sb", [P, T, N])
        xt_raw = sb("xt_raw", [P, T, KN, P])
        xt_hi = sb("xt_hi", [P, T, KN, P], f32r)
        xt_lo = sb("xt_lo", [P, T, KN, P], f32r)

        q_sb = sb("q_sb", [P, L])
        k_sb = sb("k_sb", [P, L])
        neg_max = sb("neg_max", [P, T])
        row_sum = sb("row_sum", [P, T])
        row_inv = sb("row_inv", [P, T])
        prob = sb("prob", [P, T, L])
        pt_hi = sb("pt_hi", [P, KN, L], f32r)
        pt_lo = sb("pt_lo", [P, KN, L], f32r)

        st1 = sb("st1", [P, T, 6])
        mv1 = sb("mv1", [P, T, 2])
        var1 = sb("var1", [P, T])
        rstd1 = sb("rstd1", [P, T])
        y_scale = sb("y_scale", [P, T])
        y_bias = sb("y_bias", [P, T])
        st2 = sb("st2", [P, T, 6])
        mv2 = sb("mv2", [P, T, 2])
        var2 = sb("var2", [P, T])
        rstd2 = sb("rstd2", [P, T])

        x1 = sb("x1", [P, T, N])
        zw = sb("zw", [P, T, N])
        zt_hi = sb("zt_hi", [P, 2, KN, P], f32r)
        zt_lo = sb("zt_lo", [P, 2, KN, P], f32r)
        ffn = sb("ffn", [P, 2, N])

        ps_score = [pb(f"ps_score{i}", [P, L]) for i in range(2)]
        ps_turn = [pb(f"ps_turn{i}", [P, L]) for i in range(2)]
        ps_y = [pb(f"ps_y{i}", [P, L]) for i in range(2)]
        ps_ffn = [pb(f"ps_ffn{i}", [P, N]) for i in range(2)]

        wqk_in = sem("wqk_in")
        ctx_in = sem("ctx_in")
        gates_in = sem("gates_in")
        w_in = sem("w_in")
        rows_in = sem("rows_in")
        x_in = [sem(f"x_in{t}") for t in range(T)]
        xt_in = [sem(f"xt_in{t}") for t in range(T)]
        out_stored = [sem(f"out_stored{t}") for t in range(T)]
        ident_done = sem("ident_done")
        tanh_done = sem("tanh_done")
        sign_done = sem("sign_done")
        wmax_done = sem("wmax_done")
        scale_done = sem("scale_done")
        half_done = sem("half_done")
        lnb_done = sem("lnb_done")
        gain_done = sem("gain_done")
        shift_done = sem("shift_done")
        score_ready = sem("score_ready")
        score_free = sem("score_free")
        turn_ready = sem("turn_ready")
        turn_hi = sem("turn_hi")
        turn_lo = sem("turn_lo")
        y_ready = sem("y_ready")
        y_evac = sem("y_evac")
        ffn_ready = sem("ffn_ready")
        ffn_evac = sem("ffn_evac")
        max_done = sem("max_done")
        exp_done = sem("exp_done")
        inv_done = sem("inv_done")
        prob_done = sem("prob_done")
        xt_hi_done = sem("xt_hi_done")
        xt_lo_done = sem("xt_lo_done")
        stat1 = sem("stat1")
        rstd1_done = sem("rstd1_done")
        ln1_done = sem("ln1_done")
        x1_done = sem("x1_done")
        stat2 = sem("stat2")
        rstd2_done = sem("rstd2_done")
        zw_done = sem("zw_done")
        x1b_done = sem("x1b_done")
        out_done = sem("out_done")

        STAT1 = 2 * T + 2
        STAT2 = 2 * T + 1

        def order_b(front):
            if front:
                turns = [("prob", 0), ("prob", 1), ("ffn", 0), ("ffn", 1), ("feed", 0), ("prob", 2),
                         ("prob", 3), ("feed", 1), ("ffn", 2), ("ffn", 3), ("feed", 2), ("feed", 3)]
            else:
                turns = [("ffn", 0), ("ffn", 1), ("feed", 0), ("ffn", 2), ("feed", 1), ("ffn", 3),
                         ("feed", 2), ("feed", 3)]
            plan, used, n = [], {}, 0
            for what, t in turns:
                if what == "feed":
                    plan.append((what, t, used[t]))
                else:
                    if what == "ffn":
                        used[t] = n
                    plan.append((what, t, n))
                    n += 1
            return plan

        block = es.enter_context(nc.Block())

        @block.sync
        def _(sp):
            def load_ctx(b):
                sp.dma_start(ctx_sb[:, :, :], ctx_t[b, :, :].rearrange("(k p) l -> p k l", p=P))\
                  .then_inc(ctx_in, 16)

            def load_xt(b, t):
                sp.dma_start(xt_raw[:, t, :, :], x_t[b, t, :, :, :]).then_inc(xt_in[t], 16)

            def load_x(b, t):
                sp.dma_start(x_sb[:, t, :], x[b, t * P:(t + 1) * P, :]).then_inc(x_in[t], 16)

            def store(b, t):
                sp.wait_ge(out_done, T * b + t + 1)
                sp.dma_start(out[b, t * P:(t + 1) * P, :], x1[:, t, :]).then_inc(out_stored[t], 16)

            for t in range(T):
                sp.sem_inc(out_stored[t], 16)
            sp.dma_start(wq_sb[:, :, :], wq_t.rearrange("(k p) d -> p k d", p=P)).then_inc(wqk_in, 16)
            sp.dma_start(wk_sb[:, :, :], wk_t.rearrange("(k p) d -> p k d", p=P)).then_inc(wqk_in, 16)
            load_ctx(0)
            for t in range(T):
                load_x(0, t)
            for t in range(T):
                load_xt(0, t)

            with sp.Fori(0, B - 1) as b:
                sp.wait_ge(score_ready, SCORE_USES * b + 2)
                load_ctx(b + 1)
                for t in range(T):
                    sp.wait_ge(xt_lo_done, T * b + t + 1)
                    load_xt(b + 1, t)
                for t in range(T):
                    sp.wait_ge(x1_done, T * b + t + 1)
                    load_x(b + 1, t)
                for t in range(T):
                    store(b, t)
            for t in range(T):
                store(B - 1, t)
            for t in range(T):
                sp.wait_ge(out_stored[t], 16 * (B + 1))

        @block.tensor
        def _(pe):
            def project(b):
                pe.wait_ge(ctx_in, 16 * (b + 1))
                for j, w in enumerate((wq_sb, wk_sb)):
                    n = SCORE_USES * b + j
                    if not (isinstance(b, int) and b == 0):
                        pe.wait_ge(score_free, n - 1)
                    for k in range(KC):
                        mm = pe.matmul(ps_score[j % 2][:, :], w[:, k, :], ctx_sb[:, k, :],
                                       start=(k == 0), stop=(k == KC - 1))
                    mm.then_inc(score_ready, 1)

            def scores(b, t):
                pe.wait_ge(score_free, SCORE_USES * b + (2 if t == 0 else t + 1))
                pe.matmul(ps_score[t % 2][:, :], q_sb[:, t * P:(t + 1) * P], k_sb[:, :],
                          start=True, stop=True).then_inc(score_ready, 1)

            def turn(n, bank, src):
                if not (isinstance(n, int) and n < 2):
                    pe.wait_ge(turn_lo, n - 1)
                for k in range(KN):
                    mm = pe.transpose(ps_turn[bank][:, k * P:(k + 1) * P],
                                      src[:, k * P:(k + 1) * P], ident[:, :])
                mm.then_inc(turn_ready, 1)

            def turn_prob(b, t, n, bank):
                pe.wait_ge(prob_done, T * b + t + 1)
                turn(n, bank, prob[:, t, :])

            def turn_ffn(b, t, n, bank):
                pe.wait_ge(zw_done, T * b + t + 1)
                turn(n, bank, zw[:, t, :])

            def attend(b, t):
                if t == 0:
                    pe.wait_ge(turn_lo, TURN_USES * b + T)
                pe.wait_ge(xt_lo_done, T * b + t + 1)
                if t >= 2:
                    pe.wait_ge(y_evac, T * b + t - 1)
                for k in range(KN):
                    for i, (lhs, rhs) in enumerate(((xt_hi, pt_hi), (xt_hi, pt_lo), (xt_lo, pt_hi))):
                        mm = pe.matmul(ps_y[t % 2][:, :], lhs[:, t, k, :], rhs[:, k, :],
                                       start=(k == 0 and i == 0), stop=(k == KN - 1 and i == 2))
                mm.then_inc(y_ready, 1)

            def feed(b, t, n_turn):
                pe.wait_ge(turn_lo, n_turn + 1)
                pe.wait_ge(ffn_evac, T * b + max(t, 1))
                for k in range(KN):
                    for i, lhs in enumerate((zt_hi, zt_lo)):
                        mm = pe.matmul(ps_ffn[(t + 1) % 2][:, :], lhs[:, t % 2, k, :], w_sign[:, k, :],
                                       start=(k == 0 and i == 0), stop=(k == KN - 1 and i == 1))
                mm.then_inc(ffn_ready, 1)

            def back(b, front):
                if front:
                    project(b + 1)
                for t in range(T):
                    attend(b, t)
                    if front:
                        scores(b + 1, t)
                base = TURN_USES * b + T
                for what, t, n in order_b(front):
                    if what == "prob":
                        turn_prob(b + 1, t, base + n, n % 2)
                    elif what == "ffn":
                        turn_ffn(b, t, base + n, n % 2)
                    else:
                        feed(b, t, base + n)

            pe.wait_ge(wqk_in, 32)
            project(0)
            for t in range(T):
                scores(0, t)
            pe.wait_ge(sign_done, 1)
            pe.wait_ge(lnb_done, 2)
            for k in range(KN):
                for i, lhs in enumerate((lnb_hi, lnb_lo)):
                    mm = pe.matmul(ps_ffn[0][:, :], lhs[:, k, :], w_sign[:, k, :],
                                   start=(k == 0 and i == 0), stop=(k == KN - 1 and i == 1))
            mm.then_inc(ffn_ready, 1)
            pe.wait_ge(ident_done, 2)
            for t in range(T):
                turn_prob(0, t, t, t % 2)
            with pe.Fori(0, B - 1) as b:
                back(b, True)
            back(B - 1, False)

        @block.scalar
        def _(act):
            act.dma_start(bqk[:, 0:1], bq.rearrange("(p a) -> p a", a=1)).then_inc(gates_in, 16)
            act.dma_start(bqk[:, 1:2], bk.rearrange("(p a) -> p a", a=1)).then_inc(gates_in, 16)
            act.dma_start(gates[:, 0:1], g_xattn.rearrange("(a n) -> a n", a=1).broadcast_to([P, 1]))\
               .then_inc(gates_in, 16)
            act.dma_start(gates[:, 1:2], g_ffn.rearrange("(a n) -> a n", a=1).broadcast_to([P, 1]))\
               .then_inc(gates_in, 16)
            act.dma_start(lnb_col[:, :], ln_bias_t[:, :]).then_inc(gates_in, 16)
            act.dma_start(w_raw[:, :, :], weight_t.rearrange("(k p) o -> p k o", p=P)).then_inc(w_in, 16)
            for row, dst in ((ln_weight, ln_w), (gamma, gain), (beta, shift)):
                act.dma_start(dst[:, :], row.rearrange("(a n) -> a n", a=1).broadcast_to([P, N]))\
                   .then_inc(rows_in, 16)

            def evac_qk(b):
                for j, dst in enumerate((q_sb, k_sb)):
                    act.wait_ge(score_ready, SCORE_USES * b + j + 1)
                    nc.scalar.activation(dst[:, :], ps_score[j][:, :], ACT.Identity,
                                         bias=bqk[:, j:j + 1]).then_inc(score_free, 1)

            def exps(b, t):
                act.wait_ge(max_done, T * b + t + 1)
                nc.scalar.activation(prob[:, t, :], ps_score[t % 2][:, :], ACT.Exp,
                                     bias=neg_max[:, t:t + 1], accum_out=row_sum[:, t:t + 1])\
                         .then_inc(score_free, 1)

            def normalise(b, t):
                act.wait_ge(inv_done, T * b + t + 1)
                nc.scalar.activation(prob[:, t, :], prob[:, t, :], ACT.Copy,
                                     scale=row_inv[:, t:t + 1]).then_inc(prob_done, 1)

            def split_xt(b, t):
                act.wait_ge(xt_in[t], 16 * (b + 1))
                if not (isinstance(b, int) and b == 0):
                    act.wait_ge(y_ready, T * (b - 1) + t + 1)
                nc.scalar.activation(xt_hi[:, t, :, :], xt_raw[:, t, :, :], ACT.Copy)\
                         .then_inc(xt_hi_done, 1)

            def scale_y(b, t):
                act.wait_ge(y_ready, T * b + t + 1)
                act.wait_ge(out_stored[t], 16 * (b + 1))
                if t == 0:
                    act.wait_ge(ln1_done, b + 1)
                nc.scalar.activation(x1[:, t, :], ps_y[t % 2][:, :], ACT.Identity,
                                     bias=y_bias[:, t:t + 1], scale=y_scale[:, t:t + 1])\
                         .then_inc(y_evac, 1)

            def turned_prob_hi(t, n, bank):
                act.wait_ge(turn_ready, n + 1)
                nc.scalar.activation(pt_hi[:, :, t * P:(t + 1) * P],
                                     ps_turn[bank][:, :].rearrange("p (k m) -> p k m", k=KN), ACT.Copy)\
                         .then_inc(turn_hi, 1)

            def turned_ffn_hi(t, n, bank):
                act.wait_ge(turn_ready, n + 1)
                nc.scalar.activation(zt_hi[:, t % 2, :, :],
                                     ps_turn[bank][:, :].rearrange("p (k m) -> p k m", k=KN), ACT.Copy)\
                         .then_inc(turn_hi, 1)

            def back(b, front):
                if front:
                    evac_qk(b + 1)
                for t in range(T):
                    scale_y(b, t)
                    if front:
                        if t >= 1:
                            normalise(b + 1, t - 1)
                        exps(b + 1, t)
                if front:
                    normalise(b + 1, T - 1)
                base = TURN_USES * b + T
                for what, t, n in order_b(front):
                    if what == "prob":
                        turned_prob_hi(t, base + n, n % 2)
                    elif what == "ffn":
                        turned_ffn_hi(t, base + n, n % 2)
                        if front:
                            split_xt(b + 1, t)

            act.wait_ge(gates_in, 16 * 5)
            nc.scalar.activation(tanh_g[:, :], gates[:, :], ACT.Tanh).then_inc(tanh_done, 1)
            nc.scalar.activation(lnb_hi[:, :, :], lnb_col[:, :].unsqueeze(2).broadcast_to([P, KN, P]),
                                 ACT.Copy).then_inc(lnb_done, 1)
            evac_qk(0)
            for t in range(T):
                exps(0, t)
                if t >= 1:
                    normalise(0, t - 1)
                if t == 0:
                    act.wait_ge(w_in, 16)
                    nc.scalar.activation(w_sign[:, :, :], w_raw[:, :, :], ACT.Sign).then_inc(sign_done, 1)
            normalise(0, T - 1)
            for t in range(T):
                turned_prob_hi(t, t, t % 2)
                split_xt(0, t)
            with act.Fori(0, B - 1) as b:
                back(b, True)
            back(B - 1, False)

        @block.vector
        def _(dve):
            def row_max(b, t):
                dve.wait_ge(score_ready, SCORE_USES * b + 3 + t)
                nc.vector.tensor_reduce(neg_max[:, t:t + 1], ps_score[t % 2][:, :], AX.X, ALU.max,
                                        negate=True).then_inc(max_done, 1)

            def invert(b, t):
                dve.wait_ge(score_free, SCORE_USES * b + 3 + t)
                nc.vector.reciprocal(row_inv[:, t:t + 1], row_sum[:, t:t + 1]).then_inc(inv_done, 1)

            def stats_x(b, t):
                dve.wait_ge(x_in[t], 16 * (b + 1))
                nc.vector.bn_stats(st1[:, t, :], x_sb[:, t, :]).then_inc(stat1, 1)

            def finish_stats_x(b):
                dve.drain()
                for t in range(T):
                    nc.vector.bn_aggr(mv1[:, t, :], st1[:, t, :]).then_inc(stat1, 1)
                dve.wait_ge(stat1, STAT1 * b + 2 * T)
                nc.vector.tensor_scalar(var1[:, :], mv1[:, :, 1], EPS, None, ALU.add)\
                         .then_inc(stat1, 1)
                dve.wait_ge(rstd1_done, b + 1)
                nc.vector.tensor_scalar(y_scale[:, :], rstd1[:, :], tanh_g[:, 0:1], None, ALU.mult)\
                         .then_inc(stat1, 1)
                dve.wait_ge(stat1, STAT1 * (b + 1))
                nc.vector.scalar_tensor_tensor(out=y_bias[:, :], in0=mv1[:, :, 0], scalar=-1.0,
                                               in1=y_scale[:, :], op0=ALU.mult, op1=ALU.mult)\
                         .then_inc(ln1_done, 1)

            def centre(b, t):
                dve.wait_ge(x1_done, T * b + t + 1)
                nc.vector.bn_stats(st2[:, t, :], x1[:, t, :]).then_inc(stat2, 1)
                dve.drain()
                nc.vector.bn_aggr(mv2[:, t, :], st2[:, t, :]).then_inc(stat2, 1)
                dve.wait_ge(stat2, STAT2 * b + 2 * t + 2)
                nc.vector.scalar_tensor_tensor(out=zw[:, t, :], in0=x1[:, t, :], scalar=mv2[:, t, 0:1],
                                               in1=ln_w[:, :], op0=ALU.subtract, op1=ALU.mult)\
                         .then_inc(zw_done, 1)

            def var_both(b):
                nc.vector.tensor_scalar(var2[:, :], mv2[:, :, 1], 1.0 + EPS, EPS * EPS, ALU.mult, ALU.add)\
                         .then_inc(stat2, 1)

            def turned_prob_lo(t, n, bank):
                dve.wait_ge(turn_hi, n + 1)
                cols = slice(t * P, (t + 1) * P)
                nc.vector.tensor_tensor(pt_lo[:, :, cols], ps_turn[bank][:, :].rearrange("p (k m) -> p k m", k=KN),
                                        pt_hi[:, :, cols].bitcast(f32), ALU.subtract).then_inc(turn_lo, 1)

            def turned_ffn_lo(t, n, bank):
                dve.wait_ge(turn_hi, n + 1)
                nc.vector.tensor_tensor(zt_lo[:, t % 2, :, :], ps_turn[bank][:, :].rearrange("p (k m) -> p k m", k=KN),
                                        zt_hi[:, t % 2, :, :].bitcast(f32), ALU.subtract).then_inc(turn_lo, 1)

            def scale_ffn(b, t):
                dve.wait_ge(ffn_ready, 1 + T * b + t + 1)
                if t == 0:
                    dve.wait_ge(rstd2_done, b + 1)
                if t >= 2:
                    dve.wait_ge(out_done, T * b + t - 1)
                nc.vector.scalar_tensor_tensor(out=ffn[:, t % 2, :], in0=ps_ffn[(t + 1) % 2][:, :],
                                               scalar=rstd2[:, t:t + 1], in1=gain[:, :],
                                               op0=ALU.mult, op1=ALU.mult).then_inc(ffn_evac, 1)

            def back(b, front):
                for t in range(T):
                    if front:
                        row_max(b + 1, t)
                    if t >= 1:
                        if front:
                            invert(b + 1, t - 1)
                        centre(b, t - 1)
                if front:
                    invert(b + 1, T - 1)
                centre(b, T - 1)
                dve.wait_ge(stat2, STAT2 * b + 2 * T)
                var_both(b)
                base = TURN_USES * b + T
                fed = 0
                for what, t, n in order_b(front):
                    if what == "prob":
                        turned_prob_lo(t, base + n, n % 2)
                    elif what == "ffn":
                        turned_ffn_lo(t, base + n, n % 2)
                    else:
                        scale_ffn(b, t)
                        if front:
                            stats_x(b + 1, t)
                if front:
                    finish_stats_x(b + 1)

            for t in range(T):
                stats_x(0, t)
                row_max(0, t)
                if t >= 1:
                    invert(0, t - 1)
            invert(0, T - 1)
            dve.wait_ge(lnb_done, 1)
            nc.vector.tensor_tensor(lnb_lo[:, :, :], lnb_col[:, :].unsqueeze(2).broadcast_to([P, KN, P]),
                                    lnb_hi[:, :, :].bitcast(f32), ALU.subtract).then_inc(lnb_done, 1)
            dve.wait_ge(w_in, 16)
            nc.vector.tensor_reduce(w_max[:, :], w_raw[:, :, :], AX.XY, ALU.max,
                                    apply_absolute_value=True).then_inc(wmax_done, 1)
            for t in range(T):
                turned_prob_lo(t, t, t % 2)
            dve.wait_ge(tanh_done, 1)
            finish_stats_x(0)
            dve.wait_ge(rows_in, 48)
            dve.wait_ge(scale_done, 1)
            nc.vector.tensor_scalar(gain[:, :], gain[:, :], w_scale[:, 0:1], tanh_g[:, 1:2],
                                    ALU.mult, ALU.mult).then_inc(gain_done, 1)
            dve.wait_ge(gain_done, 1)
            dve.wait_ge(ffn_ready, 1)
            nc.vector.tensor_tensor(shift_h[:, :], ps_ffn[0][:, :], gain[:, :], ALU.mult)\
                     .then_inc(ffn_evac, 1)
            dve.wait_ge(ffn_evac, 1)
            nc.vector.scalar_tensor_tensor(out=shift[:, :], in0=shift[:, :], scalar=tanh_g[:, 1:2],
                                           in1=shift_h[:, :], op0=ALU.mult, op1=ALU.add)\
                     .then_inc(shift_done, 1)
            with dve.Fori(0, B - 1) as b:
                back(b, True)
            back(B - 1, False)

        @block.gpsimd
        def _(pool):
            def split_xt(b, t):
                pool.wait_ge(xt_hi_done, T * b + t + 1)
                nc.gpsimd.tensor_tensor(xt_lo[:, t, :, :], xt_raw[:, t, :, :],
                                        xt_hi[:, t, :, :].bitcast(f32), ALU.subtract).then_inc(xt_lo_done, 1)

            def add_x(b, t):
                pool.wait_ge(y_evac, T * b + t + 1)
                pool.wait_ge(x_in[t], 16 * (b + 1))
                nc.gpsimd.tensor_tensor(x1[:, t, :], x1[:, t, :], x_sb[:, t, :], ALU.add).then_inc(x1_done, 1)

            def add_shift(b, t):
                pool.wait_ge(zw_done, T * b + t + 1)
                nc.gpsimd.tensor_tensor(x1[:, t, :], x1[:, t, :], shift[:, :], ALU.add).then_inc(x1b_done, 1)

            def add_ffn(b, t):
                pool.wait_ge(ffn_evac, 1 + T * b + t + 1)
                pool.wait_ge(x1b_done, T * b + t + 1)
                nc.gpsimd.tensor_tensor(x1[:, t, :], x1[:, t, :], ffn[:, t % 2, :], ALU.add)\
                         .then_inc(out_done, 1)

            def power1(b):
                pool.wait_ge(stat1, STAT1 * b + 2 * T + 1)
                nc.gpsimd.tensor_tensor(rstd1[:, :], var1[:, :], neg_half[:, :], ALU.pow)\
                         .then_inc(rstd1_done, 1)

            def power2(b):
                pool.wait_ge(stat2, STAT2 * (b + 1))
                pool.wait_ge(ffn_evac, 1 + T * b)
                nc.gpsimd.tensor_tensor(rstd2[:, :], var2[:, :], neg_half[:, :], ALU.pow)\
                         .then_inc(rstd2_done, 1)

            def back(b, front):
                for t in range(T):
                    add_x(b, t)
                    if t >= 1:
                        add_shift(b, t - 1)
                add_shift(b, T - 1)
                power2(b)
                for what, t, n in order_b(front):
                    if what == "ffn" and front:
                        split_xt(b + 1, t)
                    if what == "feed":
                        add_ffn(b, t)
                if front:
                    power1(b + 1)

            nc.gpsimd.memset(ident[:, :], 0.0).then_inc(ident_done, 1)
            nc.gpsimd.memset(neg_half[:, :], -0.5).then_inc(half_done, 1)
            pool.wait_ge(ident_done, 1)
            nc.gpsimd.affine_select(out=ident[:, :], in_=ident[:, :], compare_op=ALU.not_equal, fill=1.0,
                                    base=0, pattern=[[-1, P]], channel_multiplier=1).then_inc(ident_done, 1)
            pool.wait_ge(half_done, 1)
            pool.wait_ge(wmax_done, 1)
            nc.gpsimd.partition_all_reduce(w_scale[:, :], w_max[:, :], P, bass.bass_isa.ReduceOp.max)\
                     .then_inc(scale_done, 1)
            for t in range(T):
                split_xt(0, t)
            power1(0)
            pool.wait_ge(shift_done, 1)
            with pool.Fori(0, B - 1) as b:
                back(b, True)
            back(B - 1, False)


def kernel(x, ctx_1024, g_xattn, g_ffn, L0_xattn_Wq, L0_xattn_bq, L0_xattn_Wk, L0_xattn_bk,
           L0_ffn_weight, L0_ffn_gamma, L0_ffn_beta, L0_ffn_ln_weight, L0_ffn_ln_bias):
    import numpy as _np
    import concourse.bacc as _bacc
    from concourse import mybir as _mybir
    from concourse.bass_utils import run_bass_kernel_spmd as _run

    x = _np.asarray(x)
    B, L, N = x.shape
    P = 128
    x_t = x.reshape(B, L // P, P, N // P, P).transpose(0, 1, 4, 3, 2)
    feeds = {
        "x": x,
        "x_t": x_t,
        "ctx_t": _np.asarray(ctx_1024).transpose(0, 2, 1),
        "g_xattn": g_xattn,
        "g_ffn": g_ffn,
        "wq_t": _np.asarray(L0_xattn_Wq).T,
        "bq": L0_xattn_bq,
        "wk_t": _np.asarray(L0_xattn_Wk).T,
        "bk": L0_xattn_bk,
        "weight_t": _np.asarray(L0_ffn_weight).T,
        "gamma": L0_ffn_gamma,
        "beta": L0_ffn_beta,
        "ln_weight": L0_ffn_ln_weight,
        "ln_bias_t": _np.asarray(L0_ffn_ln_bias).reshape(N // P, P).T,
    }
    nc = _bacc.Bacc("TRN2", target_bir_lowering=False, num_devices=1)
    arrays, args = {}, []
    for name, a in feeds.items():
        a = _np.ascontiguousarray(a)
        arrays[f"in_{name}_dram"] = a
        args.append(nc.dram_tensor(f"in_{name}_dram", a.shape, _mybir.dt.from_np(a.dtype),
                                   kind="ExternalInput").ap())
    out = nc.dram_tensor("out_dram", (B, L, N), _mybir.dt.from_np(x.dtype), kind="ExternalOutput").ap()
    flamingo_block_kernel(nc, *args, out)
    r = _run(nc, [arrays], core_ids=[0])
    return r.results[0]["out_dram"]
```

```python
import concourse.bass as bass
from concourse import mybir
from contextlib import ExitStack


def flamingo_block_kernel(nc, x, x_t, ctx_t, g_xattn, g_ffn, wq_t, bq, wk_t, bk,
                          weight_t, gamma, beta, ln_weight, ln_bias_t, out):
    f32 = mybir.dt.float32
    f32r = mybir.dt.float32r
    ALU = mybir.AluOpType
    ACT = mybir.ActivationFunctionType
    AX = mybir.AxisListType

    P = 128
    B, L, N = x.shape
    C = ctx_t.shape[1]
    D = wq_t.shape[1]
    T = L // P
    KN = N // P
    KC = C // P
    EPS = 1e-5

    HALF = T // 2

    es = ExitStack()
    with es:
        def sb(name, shape, dt=f32):
            return es.enter_context(nc.sbuf_tensor(name, shape, dt))

        def pb(name, shape):
            return es.enter_context(nc.psum_tensor(name, shape, f32))

        def sem(name):
            return es.enter_context(nc.semaphore(name))

        wq_sb = sb("wq_sb", [P, KC, D])
        wk_sb = sb("wk_sb", [P, KC, D])
        bqk = sb("bqk", [P, 2])
        w_raw = sb("w_raw", [P, KN, N])
        w_sign = sb("w_sign", [P, KN, N], f32r)
        ln_w = sb("ln_w", [P, N])
        gain = sb("gain", [P, N])
        shift = sb("shift", [P, N])
        shift_h = sb("shift_h", [P, N])
        lnb_col = sb("lnb_col", [P, KN])
        lnb_hi = sb("lnb_hi", [P, KN, P], f32r)
        lnb_lo = sb("lnb_lo", [P, KN, P], f32r)
        gates = sb("gates", [P, 2])
        tanh_g = sb("tanh_g", [P, 2])
        w_max = sb("w_max", [P, 1])
        w_scale = sb("w_scale", [P, 1])
        ident = sb("ident", [P, P])
        neg_half = sb("neg_half", [P, T])

        ctx_sb = sb("ctx_sb", [P, B, KC, L])
        x_sb = sb("x_sb", [P, T, N])
        xt_raw = sb("xt_raw", [P, T, KN, P])
        xt_hi = sb("xt_hi", [P, T, KN, P], f32r)
        xt_lo = sb("xt_lo", [P, T, KN, P], f32r)

        q_hi = sb("q_hi", [P, L], f32r)
        q_lo = sb("q_lo", [P, L], f32r)
        q_hi_later = sb("q_hi_later", [P, B, L], f32r)
        q_lo_later = sb("q_lo_later", [P, B, L], f32r)
        k_hi = sb("k_hi", [P, B, L], f32r)
        k_lo = sb("k_lo", [P, B, L], f32r)
        neg_max = sb("neg_max", [P, T])
        row_sum = sb("row_sum", [P, T])
        row_inv = sb("row_inv", [P, T])
        prob = sb("prob", [P, T, L])
        pt_hi = sb("pt_hi", [P, KN, L], f32r)
        pt_lo = sb("pt_lo", [P, KN, L], f32r)

        unread = sb("unread", [P, 2, N])
        neg_mean1 = sb("neg_mean1", [P, T])
        sq_sum1 = sb("sq_sum1", [P, T])
        var1 = sb("var1", [P, T])
        rstd1 = sb("rstd1", [P, T])
        y_scale = sb("y_scale", [P, T])
        y_bias = sb("y_bias", [P, T])
        st2 = sb("st2", [P, T, 6])
        mv2 = sb("mv2", [P, T, 2])
        var2 = sb("var2", [P, T])
        rstd2 = sb("rstd2", [P, T])

        x1 = sb("x1", [P, T, N])
        zw = sb("zw", [P, T, N])
        zt_hi = sb("zt_hi", [P, 2, KN, P], f32r)
        zt_lo = sb("zt_lo", [P, 2, KN, P], f32r)
        ffn = sb("ffn", [P, 2, N])

        ps_score = [pb(f"ps_score{i}", [P, L]) for i in range(2)]
        ps_turn = [pb(f"ps_turn{i}", [P, L]) for i in range(2)]
        ps_y = [pb(f"ps_y{i}", [P, L]) for i in range(2)]
        ps_ffn = [pb(f"ps_ffn{i}", [P, N]) for i in range(2)]

        wqk_in = sem("wqk_in")
        ctx_in = [sem(f"ctx_in{b}") for b in range(B)]
        gates_in = sem("gates_in")
        w_in = sem("w_in")
        rows_in = sem("rows_in")
        x_in = [sem(f"x_in{t}") for t in range(T)]
        xt_in = [sem(f"xt_in{t}") for t in range(T)]
        out_stored = [sem(f"out_stored{t}") for t in range(T)]
        ident_done = sem("ident_done")
        tanh_done = sem("tanh_done")
        sign_done = sem("sign_done")
        wmax_done = sem("wmax_done")
        scale_done = sem("scale_done")
        half_done = sem("half_done")
        lnb_done = sem("lnb_done")
        gain_done = sem("gain_done")
        shift_done = sem("shift_done")
        proj_ready = sem("proj_ready")
        proj_hi = sem("proj_hi")
        proj_lo = sem("proj_lo")
        q_moved = sem("q_moved")
        score_ready = sem("score_ready")
        pt_ready = sem("pt_ready")
        pt_hi_done = sem("pt_hi_done")
        pt_lo_done = sem("pt_lo_done")
        zt_ready = sem("zt_ready")
        zt_hi_done = sem("zt_hi_done")
        zt_lo_done = sem("zt_lo_done")
        y_ready = sem("y_ready")
        ffn_ready = sem("ffn_ready")
        ffn_evac = sem("ffn_evac")
        max_done = sem("max_done")
        exp_done = sem("exp_done")
        inv_done = sem("inv_done")
        prob_done = sem("prob_done")
        xt_hi_done = sem("xt_hi_done")
        xt_lo_done = sem("xt_lo_done")
        mean1_done = sem("mean1_done")
        square1_done = sem("square1_done")
        var1_done = sem("var1_done")
        scale1_done = sem("scale1_done")
        x_biased = sem("x_biased")
        later_zeroed = sem("later_zeroed")
        rstd1_done = sem("rstd1_done")
        ln1_done = sem("ln1_done")
        x1_done = sem("x1_done")
        stat2 = sem("stat2")
        rstd2_done = sem("rstd2_done")
        zw_done = sem("zw_done")
        x1b_done = sem("x1b_done")
        out_done = sem("out_done")

        STAT2 = 2 * T + 2

        block = es.enter_context(nc.Block())

        turn_first = (ps_y[0], ps_y[1], ps_turn[0], ps_turn[1])
        turn_later = (ps_score[0], ps_score[1], ps_y[0], ps_y[1])

        @block.sync
        def _(sp):
            def load_ctx(b):
                sp.dma_start(ctx_sb[:, b, :, :], ctx_t[b, :, :].rearrange("(k p) l -> p k l", p=P))\
                  .then_inc(ctx_in[b], 16)

            def load_xt(b, t):
                sp.dma_start(xt_raw[:, t, :, :], x_t[b, t, :, :, :]).then_inc(xt_in[t], 16)

            def load_x(b, t):
                sp.dma_start(x_sb[:, t, :], x[b, t * P:(t + 1) * P, :]).then_inc(x_in[t], 16)

            def store(b, t):
                sp.wait_ge(out_done, T * b + t + 1)
                sp.dma_start(out[b, t * P:(t + 1) * P, :], x1[:, t, :]).then_inc(out_stored[t], 16)

            for t in range(T):
                sp.sem_inc(out_stored[t], 16)
            sp.dma_start(wq_sb[:, :, :], wq_t.rearrange("(k p) d -> p k d", p=P)).then_inc(wqk_in, 16)
            sp.dma_start(wk_sb[:, :, :], wk_t.rearrange("(k p) d -> p k d", p=P)).then_inc(wqk_in, 16)
            load_ctx(0)
            for t in range(T):
                load_x(0, t)
            load_ctx(1)
            for t in range(T):
                load_xt(0, t)
            sp.dma_start(w_raw[:, :, :], weight_t.rearrange("(k p) o -> p k o", p=P)).then_inc(w_in, 16)
            for b in range(2, B):
                load_ctx(b)

            with sp.Fori(0, B - 1) as b:
                for t in range(T):
                    sp.wait_ge(x1_done, T * b + t + 1)
                    load_x(b + 1, t)
                    sp.wait_ge(xt_lo_done, T * b + t + 1)
                    load_xt(b + 1, t)
                for t in range(T):
                    store(b, t)
            for t in range(T):
                store(B - 1, t)
            for t in range(T):
                sp.wait_ge(out_stored[t], 16 * (B + 1))

        @block.tensor
        def _(pe):
            def project(b):
                pe.wait_ge(ctx_in[b], 16)
                for j, w in enumerate((wq_sb, wk_sb)):
                    if b in (1, 2):
                        pe.wait_ge(exp_done, 2 * (b - 1) + j + 1)
                    elif b > 2:
                        pe.wait_ge(proj_lo, 2 * (b - 1) + j + 1)
                    for k in range(KC):
                        mm = pe.matmul(ps_score[j][:, :], w[:, k, :], ctx_sb[:, b, k, :],
                                       start=(k == 0), stop=(k == KC - 1))
                    mm.then_inc(proj_ready, 1)

            def scores(b, t, first):
                if first and t < 2:
                    pe.wait_ge(proj_lo, 2)
                elif first:
                    pe.wait_ge(proj_lo, t + 1)
                elif t == 0:
                    pe.wait_ge(q_moved, 2 * b)
                elif t >= 2:
                    pe.wait_ge(exp_done, T * b + t - 1)
                for i, (lhs, rhs) in enumerate(((q_hi, k_hi), (q_hi, k_lo), (q_lo, k_hi))):
                    mm = pe.matmul(ps_score[t % 2][:, :], lhs[:, t * P:(t + 1) * P], rhs[:, b, :],
                                   start=(i == 0), stop=(i == 2))
                mm.then_inc(score_ready, 1)

            def turn(bank, src, ready):
                for k in range(KN):
                    mm = pe.transpose(bank[:, k * P:(k + 1) * P], src[:, k * P:(k + 1) * P], ident[:, :])
                mm.then_inc(ready, 1)

            def turn_prob(b, t, first=False):
                pe.wait_ge(prob_done, T * b + t + 1)
                if not first:
                    if t < 2:
                        pe.wait_ge(exp_done, T * b + t + 3)
                    else:
                        pe.wait_ge(x1_done, T * (b - 1) + t + 1)
                turn((turn_first if first else turn_later)[t], prob[:, t, :], pt_ready)

            def turn_ffn(b, t):
                pe.wait_ge(zw_done, T * b + t + 1)
                turn(ps_turn[t % 2], zw[:, t, :], zt_ready)

            def attend(b, t):
                if t == 0:
                    pe.wait_ge(pt_lo_done, T * (b + 1))
                pe.wait_ge(xt_lo_done, T * b + t + 1)
                if t >= 2:
                    pe.wait_ge(x1_done, T * b + t - 1)
                for k in range(KN):
                    for i, (lhs, rhs) in enumerate(((xt_hi, pt_hi), (xt_hi, pt_lo), (xt_lo, pt_hi))):
                        mm = pe.matmul(ps_y[t % 2][:, :], lhs[:, t, k, :], rhs[:, k, :],
                                       start=(k == 0 and i == 0), stop=(k == KN - 1 and i == 2))
                mm.then_inc(y_ready, 1)

            def feed(b, t):
                pe.wait_ge(zt_lo_done, T * b + t + 1)
                pe.wait_ge(ffn_evac, T * b + max(t, 1))
                for k in range(KN):
                    for i, lhs in enumerate((zt_hi, zt_lo)):
                        mm = pe.matmul(ps_ffn[(t + 1) % 2][:, :], lhs[:, t % 2, k, :], w_sign[:, k, :],
                                       start=(k == 0 and i == 0), stop=(k == KN - 1 and i == 1))
                mm.then_inc(ffn_ready, 1)

            def back(b, front):
                if front:
                    scores(b + 1, 0, False)
                attend(b, 1)
                if front:
                    scores(b + 1, 1, False)
                turn_ffn(b, 0)
                attend(b, 2)
                turn_ffn(b, 1)
                if front:
                    scores(b + 1, 2, False)
                    scores(b + 1, 3, False)
                feed(b, 0)
                attend(b, 3)
                if front:
                    turn_prob(b + 1, 0)
                    turn_prob(b + 1, 1)
                    turn_prob(b + 1, 2)
                turn_ffn(b, 2)
                feed(b, 1)
                if front:
                    turn_prob(b + 1, 3)
                feed(b, 2)
                turn_ffn(b, 3)
                if front:
                    attend(b + 1, 0)
                feed(b, 3)

            pe.wait_ge(wqk_in, 32)
            project(0)
            scores(0, 0, True)
            scores(0, 1, True)
            project(1)
            scores(0, 2, True)
            scores(0, 3, True)
            pe.wait_ge(ident_done, 2)
            project(2)
            turn_prob(0, 0, True)
            turn_prob(0, 1, True)
            project(3)
            turn_prob(0, 2, True)
            turn_prob(0, 3, True)
            pe.wait_ge(sign_done, 1)
            pe.wait_ge(lnb_done, 2)
            for k in range(KN):
                for i, lhs in enumerate((lnb_hi, lnb_lo)):
                    mm = pe.matmul(ps_ffn[0][:, :], lhs[:, k, :], w_sign[:, k, :],
                                   start=(k == 0 and i == 0), stop=(k == KN - 1 and i == 1))
            mm.then_inc(ffn_ready, 1)
            pe.wait_ge(proj_lo, 2 * B)
            attend(0, 0)
            with pe.Fori(0, B - 1) as b:
                back(b, True)
            back(B - 1, False)

        @block.scalar
        def _(act):
            act.dma_start(bqk[:, 0:1], bq.rearrange("(p a) -> p a", a=1)).then_inc(gates_in, 16)
            act.dma_start(bqk[:, 1:2], bk.rearrange("(p a) -> p a", a=1)).then_inc(gates_in, 16)
            act.dma_start(gates[:, 0:1], g_xattn.rearrange("(a n) -> a n", a=1).broadcast_to([P, 1]))\
               .then_inc(gates_in, 16)
            act.dma_start(gates[:, 1:2], g_ffn.rearrange("(a n) -> a n", a=1).broadcast_to([P, 1]))\
               .then_inc(gates_in, 16)
            act.dma_start(lnb_col[:, :], ln_bias_t[:, :]).then_inc(gates_in, 16)
            for row, dst in ((ln_weight, ln_w), (gamma, gain), (beta, shift)):
                act.dma_start(dst[:, :], row.rearrange("(a n) -> a n", a=1).broadcast_to([P, N]))\
                   .then_inc(rows_in, 16)

            def round_qk(b):
                for j, dst in enumerate((q_hi[:, :] if b == 0 else q_hi_later[:, b - 1, :], k_hi[:, b, :])):
                    act.wait_ge(proj_ready, 2 * b + j + 1)
                    nc.scalar.activation(dst, ps_score[j][:, :], ACT.Identity,
                                         bias=bqk[:, j:j + 1]).then_inc(proj_hi, 1)

            def exps(b, t):
                act.wait_ge(max_done, T * b + t + 1)
                nc.scalar.activation(prob[:, t, :], ps_score[t % 2][:, :], ACT.Exp,
                                     bias=neg_max[:, t:t + 1], accum_out=row_sum[:, t:t + 1])\
                         .then_inc(exp_done, 1)

            def normalise(b, t):
                act.wait_ge(inv_done, T * b + t + 1)
                nc.scalar.activation(prob[:, t, :], prob[:, t, :], ACT.Copy,
                                     scale=row_inv[:, t:t + 1]).then_inc(prob_done, 1)

            def split_xt(b, t):
                act.wait_ge(xt_in[t], 16 * (b + 1))
                act.wait_ge(y_ready, T * (b - 1) + t + 1)
                nc.scalar.activation(xt_hi[:, t, :, :], xt_raw[:, t, :, :], ACT.Copy)\
                         .then_inc(xt_hi_done, 1)

            def stats_x(b, t):
                act.wait_ge(x_in[t], 16 * (b + 1))
                nc.scalar.activation(unread[:, 0, :], x_sb[:, t, :], ACT.Copy, scale=-1.0 / N,
                                     accum_out=neg_mean1[:, t:t + 1]).then_inc(mean1_done, 1)
                act.wait_ge(mean1_done, T * b + t + 1)
                if not (isinstance(b, int) and b == 0 and t == 0):
                    act.wait_ge(square1_done, T * b + t)
                nc.scalar.activation(unread[:, 1, :], x_sb[:, t, :], ACT.Square, bias=neg_mean1[:, t:t + 1],
                                     accum_out=sq_sum1[:, t:t + 1]).then_inc(square1_done, 1)

            def bias_x(b):
                act.wait_ge(ln1_done, b + 1)
                for t in range(T):
                    nc.scalar.activation(x_sb[:, t, :], x_sb[:, t, :], ACT.Identity,
                                         bias=y_bias[:, t:t + 1]).then_inc(x_biased, 1)

            def turned_prob_hi(b, t, first=False):
                act.wait_ge(pt_ready, T * b + t + 1)
                bank = (turn_first if first else turn_later)[t]
                nc.scalar.activation(pt_hi[:, :, t * P:(t + 1) * P],
                                     bank[:, :].rearrange("p (k m) -> p k m", k=KN), ACT.Copy)\
                         .then_inc(pt_hi_done, 1)

            def turned_ffn_hi(b, t):
                act.wait_ge(zt_ready, T * b + t + 1)
                nc.scalar.activation(zt_hi[:, t % 2, :, :],
                                     ps_turn[t % 2][:, :].rearrange("p (k m) -> p k m", k=KN), ACT.Copy)\
                         .then_inc(zt_hi_done, 1)

            def back(b, front):
                if front:
                    exps(b + 1, 0)
                    normalise(b + 1, 0)
                    exps(b + 1, 1)
                turned_ffn_hi(b, 0)
                if front:
                    normalise(b + 1, 1)
                turned_ffn_hi(b, 1)
                if front:
                    stats_x(b + 1, 0)
                    split_xt(b + 1, 0)
                    exps(b + 1, 2)
                    exps(b + 1, 3)
                    stats_x(b + 1, 1)
                    normalise(b + 1, 2)
                    normalise(b + 1, 3)
                    split_xt(b + 1, 1)
                    turned_prob_hi(b + 1, 0)
                    turned_prob_hi(b + 1, 1)
                    turned_prob_hi(b + 1, 2)
                turned_ffn_hi(b, 2)
                if front:
                    stats_x(b + 1, 2)
                    turned_prob_hi(b + 1, 3)
                    stats_x(b + 1, 3)
                turned_ffn_hi(b, 3)
                if front:
                    bias_x(b + 1)
                    split_xt(b + 1, 2)
                    split_xt(b + 1, 3)

            act.wait_ge(gates_in, 16 * 5)
            nc.scalar.activation(tanh_g[:, :], gates[:, :], ACT.Tanh).then_inc(tanh_done, 1)
            nc.scalar.activation(lnb_hi[:, :, :], lnb_col[:, :].unsqueeze(2).broadcast_to([P, KN, P]),
                                 ACT.Copy).then_inc(lnb_done, 1)
            stats_x(0, 0)
            round_qk(0)
            stats_x(0, 1)
            exps(0, 0)
            exps(0, 1)
            stats_x(0, 2)
            normalise(0, 0)
            round_qk(1)
            normalise(0, 1)
            exps(0, 2)
            exps(0, 3)
            stats_x(0, 3)
            round_qk(2)
            normalise(0, 2)
            turned_prob_hi(0, 0, True)
            normalise(0, 3)
            turned_prob_hi(0, 1, True)
            round_qk(3)
            turned_prob_hi(0, 2, True)
            turned_prob_hi(0, 3, True)
            bias_x(0)
            act.wait_ge(w_in, 16)
            nc.scalar.activation(w_sign[:, :, :], w_raw[:, :, :], ACT.Sign).then_inc(sign_done, 1)
            with act.Fori(0, B - 1) as b:
                back(b, True)
            back(B - 1, False)

        @block.vector
        def _(dve):
            def row_max(b, t):
                dve.wait_ge(score_ready, T * b + t + 1)
                nc.vector.tensor_reduce(neg_max[:, t:t + 1], ps_score[t % 2][:, :], AX.X, ALU.max,
                                        negate=True).then_inc(max_done, 1)

            def invert(b, t):
                dve.wait_ge(exp_done, T * b + t + 1)
                nc.vector.reciprocal(row_inv[:, t:t + 1], row_sum[:, t:t + 1]).then_inc(inv_done, 1)

            def rest_qk(b):
                dst = (q_lo[:, :] if b == 0 else q_lo_later[:, b - 1, :], k_lo[:, b, :])
                hi = (q_hi[:, :] if b == 0 else q_hi_later[:, b - 1, :], k_hi[:, b, :])
                for j in range(2):
                    dve.wait_ge(proj_hi, 2 * b + j + 1)
                    nc.vector.scalar_tensor_tensor(out=dst[j], in0=ps_score[j][:, :], scalar=bqk[:, j:j + 1],
                                                   in1=hi[j].bitcast(f32), op0=ALU.add, op1=ALU.subtract)\
                             .then_inc(proj_lo, 1)

            def move_q(b):
                nc.vector.tensor_copy(q_hi[:, :], q_hi_later[:, b, :]).then_inc(q_moved, 1)
                nc.vector.tensor_copy(q_lo[:, :], q_lo_later[:, b, :]).then_inc(q_moved, 1)

            def var_x(b):
                dve.wait_ge(square1_done, T * (b + 1))
                nc.vector.tensor_scalar(var1[:, :], sq_sum1[:, :], 1.0 / N, EPS, ALU.mult, ALU.add)\
                         .then_inc(var1_done, 1)

            def scale_x(b):
                dve.wait_ge(rstd1_done, b + 1)
                nc.vector.tensor_scalar(y_scale[:, :], rstd1[:, :], tanh_g[:, 0:1], None, ALU.mult)\
                         .then_inc(scale1_done, 1)
                dve.wait_ge(scale1_done, b + 1)
                nc.vector.tensor_tensor(y_bias[:, :], neg_mean1[:, :], y_scale[:, :], ALU.mult)\
                         .then_inc(ln1_done, 1)

            def add_y(b, t):
                dve.wait_ge(out_stored[t], 16 * (b + 1))
                dve.wait_ge(x_biased, T * b + t + 1)
                dve.wait_ge(y_ready, T * b + t + 1)
                nc.vector.scalar_tensor_tensor(out=x1[:, t, :], in0=ps_y[t % 2][:, :],
                                               scalar=y_scale[:, t:t + 1], in1=x_sb[:, t, :],
                                               op0=ALU.mult, op1=ALU.add).then_inc(x1_done, 1)

            def mean_x1(b, t):
                dve.wait_ge(x1_done, T * b + t + 1)
                nc.vector.bn_stats(st2[:, t, :], x1[:, t, :]).then_inc(stat2, 1)
                dve.drain()
                nc.vector.bn_aggr(mv2[:, t, :], st2[:, t, :]).then_inc(stat2, 1)

            def centre(b, t):
                dve.wait_ge(stat2, STAT2 * b + 2 * t + 2 + t // HALF)
                nc.vector.scalar_tensor_tensor(out=zw[:, t, :], in0=x1[:, t, :], scalar=mv2[:, t, 0:1],
                                               in1=ln_w[:, :], op0=ALU.subtract, op1=ALU.mult)\
                         .then_inc(zw_done, 1)

            def var_both(b, half):
                cols = slice(half * HALF, (half + 1) * HALF)
                nc.vector.tensor_scalar(var2[:, cols], mv2[:, cols, 1], 1.0 + EPS, EPS * EPS,
                                        ALU.mult, ALU.add).then_inc(stat2, 1)

            def turned_prob_lo(b, t, first=False):
                dve.wait_ge(pt_hi_done, T * b + t + 1)
                bank = (turn_first if first else turn_later)[t]
                cols = slice(t * P, (t + 1) * P)
                nc.vector.tensor_tensor(pt_lo[:, :, cols], bank[:, :].rearrange("p (k m) -> p k m", k=KN),
                                        pt_hi[:, :, cols].bitcast(f32), ALU.subtract).then_inc(pt_lo_done, 1)

            def turned_ffn_lo(b, t):
                dve.wait_ge(zt_hi_done, T * b + t + 1)
                nc.vector.tensor_tensor(zt_lo[:, t % 2, :, :],
                                        ps_turn[t % 2][:, :].rearrange("p (k m) -> p k m", k=KN),
                                        zt_hi[:, t % 2, :, :].bitcast(f32), ALU.subtract).then_inc(zt_lo_done, 1)

            def scale_ffn(b, t):
                dve.wait_ge(ffn_ready, 1 + T * b + t + 1)
                if t % HALF == 0:
                    dve.wait_ge(rstd2_done, 2 * b + t // HALF + 1)
                if t >= 2:
                    dve.wait_ge(out_done, T * b + t - 1)
                nc.vector.scalar_tensor_tensor(out=ffn[:, t % 2, :], in0=ps_ffn[(t + 1) % 2][:, :],
                                               scalar=rstd2[:, t:t + 1], in1=gain[:, :],
                                               op0=ALU.mult, op1=ALU.mult).then_inc(ffn_evac, 1)

            def back(b, front):
                if front:
                    row_max(b + 1, 0)
                mean_x1(b, 0)
                centre(b, 0)
                if front:
                    invert(b + 1, 0)
                add_y(b, 1)
                if front:
                    row_max(b + 1, 1)
                mean_x1(b, 1)
                centre(b, 1)
                if front:
                    invert(b + 1, 1)
                var_both(b, 0)
                turned_ffn_lo(b, 0)
                add_y(b, 2)
                if front:
                    row_max(b + 1, 2)
                turned_ffn_lo(b, 1)
                mean_x1(b, 2)
                if front:
                    row_max(b + 1, 3)
                    invert(b + 1, 2)
                centre(b, 2)
                if front:
                    invert(b + 1, 3)
                    move_q(b + 1)
                scale_ffn(b, 0)
                add_y(b, 3)
                mean_x1(b, 3)
                if front:
                    turned_prob_lo(b + 1, 0)
                centre(b, 3)
                var_both(b, 1)
                if front:
                    turned_prob_lo(b + 1, 1)
                turned_ffn_lo(b, 2)
                if front:
                    turned_prob_lo(b + 1, 2)
                    turned_prob_lo(b + 1, 3)
                scale_ffn(b, 1)
                if front:
                    var_x(b + 1)
                turned_ffn_lo(b, 3)
                if front:
                    scale_x(b + 1)
                scale_ffn(b, 2)
                if front:
                    add_y(b + 1, 0)
                scale_ffn(b, 3)

            dve.wait_ge(gates_in, 16 * 5)
            rest_qk(0)
            row_max(0, 0)
            row_max(0, 1)
            invert(0, 0)
            rest_qk(1)
            invert(0, 1)
            row_max(0, 2)
            row_max(0, 3)
            invert(0, 2)
            rest_qk(2)
            invert(0, 3)
            var_x(0)
            turned_prob_lo(0, 0, True)
            turned_prob_lo(0, 1, True)
            rest_qk(3)
            dve.wait_ge(tanh_done, 1)
            scale_x(0)
            dve.wait_ge(later_zeroed, 2)
            move_q(0)
            turned_prob_lo(0, 2, True)
            turned_prob_lo(0, 3, True)
            dve.wait_ge(lnb_done, 1)
            nc.vector.tensor_tensor(lnb_lo[:, :, :], lnb_col[:, :].unsqueeze(2).broadcast_to([P, KN, P]),
                                    lnb_hi[:, :, :].bitcast(f32), ALU.subtract).then_inc(lnb_done, 1)
            dve.wait_ge(w_in, 16)
            nc.vector.tensor_reduce(w_max[:, :], w_raw[:, :, :], AX.XY, ALU.max,
                                    apply_absolute_value=True).then_inc(wmax_done, 1)
            dve.wait_ge(rows_in, 48)
            dve.wait_ge(scale_done, 1)
            nc.vector.tensor_scalar(gain[:, :], gain[:, :], w_scale[:, 0:1], tanh_g[:, 1:2],
                                    ALU.mult, ALU.mult).then_inc(gain_done, 1)
            dve.wait_ge(gain_done, 1)
            dve.wait_ge(ffn_ready, 1)
            nc.vector.tensor_tensor(shift_h[:, :], ps_ffn[0][:, :], gain[:, :], ALU.mult)\
                     .then_inc(ffn_evac, 1)
            dve.wait_ge(ffn_evac, 1)
            nc.vector.scalar_tensor_tensor(out=shift[:, :], in0=shift[:, :], scalar=tanh_g[:, 1:2],
                                           in1=shift_h[:, :], op0=ALU.mult, op1=ALU.add)\
                     .then_inc(shift_done, 1)
            add_y(0, 0)
            with dve.Fori(0, B - 1) as b:
                back(b, True)
            back(B - 1, False)

        @block.gpsimd
        def _(pool):
            def split_xt(b, t):
                pool.wait_ge(xt_hi_done, T * b + t + 1)
                nc.gpsimd.tensor_tensor(xt_lo[:, t, :, :], xt_raw[:, t, :, :],
                                        xt_hi[:, t, :, :].bitcast(f32), ALU.subtract).then_inc(xt_lo_done, 1)

            def add_shift(b, t):
                pool.wait_ge(zw_done, T * b + t + 1)
                nc.gpsimd.tensor_tensor(x1[:, t, :], x1[:, t, :], shift[:, :], ALU.add).then_inc(x1b_done, 1)

            def add_ffn(b, t):
                pool.wait_ge(ffn_evac, 1 + T * b + t + 1)
                pool.wait_ge(x1b_done, T * b + t + 1)
                nc.gpsimd.tensor_tensor(x1[:, t, :], x1[:, t, :], ffn[:, t % 2, :], ALU.add)\
                         .then_inc(out_done, 1)

            def power1(b):
                pool.wait_ge(var1_done, b + 1)
                nc.gpsimd.tensor_tensor(rstd1[:, :], var1[:, :], neg_half[:, :], ALU.pow)\
                         .then_inc(rstd1_done, 1)

            def power2(b, half):
                pool.wait_ge(stat2, STAT2 * b + (half + 1) * (2 * HALF + 1))
                cols = slice(half * HALF, (half + 1) * HALF)
                nc.gpsimd.tensor_tensor(rstd2[:, cols], var2[:, cols], neg_half[:, cols], ALU.pow)\
                         .then_inc(rstd2_done, 1)

            def back(b, front):
                add_shift(b, 0)
                add_shift(b, 1)
                power2(b, 0)
                if front:
                    split_xt(b + 1, 0)
                add_shift(b, 2)
                if front:
                    split_xt(b + 1, 1)
                add_ffn(b, 0)
                power2(b, 1)
                add_shift(b, 3)
                add_ffn(b, 1)
                if front:
                    power1(b + 1)
                add_ffn(b, 2)
                add_ffn(b, 3)
                if front:
                    split_xt(b + 1, 2)
                    split_xt(b + 1, 3)

            nc.gpsimd.memset(ident[:, :], 0.0).then_inc(ident_done, 1)
            for later in (q_hi_later, q_lo_later):
                nc.gpsimd.memset(later[:, B - 1, :].bitcast(f32), 0.0).then_inc(later_zeroed, 1)
            nc.gpsimd.memset(neg_half[:, :], -0.5).then_inc(half_done, 1)
            pool.wait_ge(ident_done, 1)
            nc.gpsimd.affine_select(out=ident[:, :], in_=ident[:, :], compare_op=ALU.not_equal, fill=1.0,
                                    base=0, pattern=[[-1, P]], channel_multiplier=1).then_inc(ident_done, 1)
            for t in range(T):
                pool.wait_ge(xt_in[t], 16)
                nc.gpsimd.tensor_copy(xt_hi[:, t, :, :], xt_raw[:, t, :, :]).then_inc(xt_hi_done, 1)
                split_xt(0, t)
            pool.wait_ge(half_done, 1)
            power1(0)
            pool.wait_ge(wmax_done, 1)
            nc.gpsimd.partition_all_reduce(w_scale[:, :], w_max[:, :], P, bass.bass_isa.ReduceOp.max)\
                     .then_inc(scale_done, 1)
            pool.wait_ge(shift_done, 1)
            with pool.Fori(0, B - 1) as b:
                back(b, True)
            back(B - 1, False)


def kernel(x, ctx_1024, g_xattn, g_ffn, L0_xattn_Wq, L0_xattn_bq, L0_xattn_Wk, L0_xattn_bk,
           L0_ffn_weight, L0_ffn_gamma, L0_ffn_beta, L0_ffn_ln_weight, L0_ffn_ln_bias):
    import numpy as _np
    import concourse.bacc as _bacc
    from concourse import mybir as _mybir
    from concourse.bass_utils import run_bass_kernel_spmd as _run

    x = _np.asarray(x)
    B, L, N = x.shape
    P = 128
    x_t = x.reshape(B, L // P, P, N // P, P).transpose(0, 1, 4, 3, 2)
    feeds = {
        "x": x,
        "x_t": x_t,
        "ctx_t": _np.asarray(ctx_1024).transpose(0, 2, 1),
        "g_xattn": g_xattn,
        "g_ffn": g_ffn,
        "wq_t": _np.asarray(L0_xattn_Wq).T,
        "bq": L0_xattn_bq,
        "wk_t": _np.asarray(L0_xattn_Wk).T,
        "bk": L0_xattn_bk,
        "weight_t": _np.asarray(L0_ffn_weight).T,
        "gamma": L0_ffn_gamma,
        "beta": L0_ffn_beta,
        "ln_weight": L0_ffn_ln_weight,
        "ln_bias_t": _np.asarray(L0_ffn_ln_bias).reshape(N // P, P).T,
    }
    nc = _bacc.Bacc("TRN2", target_bir_lowering=False, num_devices=1)
    arrays, args = {}, []
    for name, a in feeds.items():
        a = _np.ascontiguousarray(a)
        arrays[f"in_{name}_dram"] = a
        args.append(nc.dram_tensor(f"in_{name}_dram", a.shape, _mybir.dt.from_np(a.dtype),
                                   kind="ExternalInput").ap())
    out = nc.dram_tensor("out_dram", (B, L, N), _mybir.dt.from_np(x.dtype), kind="ExternalOutput").ap()
    flamingo_block_kernel(nc, *args, out)
    r = _run(nc, [arrays], core_ids=[0])
    return r.results[0]["out_dram"]
```

```python
import concourse.bass as bass
from concourse import mybir
from contextlib import ExitStack


def flamingo_block_kernel(nc, x, x_t, ctx_t, g_xattn, g_ffn, wq_t, bq, wk_t, bk,
                          weight_t, gamma, beta, ln_weight, ln_bias_t, out):
    f32 = mybir.dt.float32
    f32r = mybir.dt.float32r
    ALU = mybir.AluOpType
    ACT = mybir.ActivationFunctionType
    AX = mybir.AxisListType

    P = 128
    B, L, N = x.shape
    C = ctx_t.shape[1]
    D = wq_t.shape[1]
    T = L // P
    KN = N // P
    KC = C // P
    EPS = 1e-5
    WHOLE = 2
    WARM = 7

    HALF = T // 2

    es = ExitStack()
    with es:
        def sb(name, shape, dt=f32):
            return es.enter_context(nc.sbuf_tensor(name, shape, dt))

        def pb(name, shape):
            return es.enter_context(nc.psum_tensor(name, shape, f32))

        def sem(name):
            return es.enter_context(nc.semaphore(name))

        wq_sb = sb("wq_sb", [P, KC, D])
        wk_sb = sb("wk_sb", [P, KC, D])
        wq_hi = sb("wq_hi", [P, KC, D], f32r)
        wq_lo = sb("wq_lo", [P, KC, D], f32r)
        wk_hi = sb("wk_hi", [P, KC, D], f32r)
        wk_lo = sb("wk_lo", [P, KC, D], f32r)
        bqk = sb("bqk", [P, 2])
        w_raw = sb("w_raw", [P, KN, N])
        w_sign = sb("w_sign", [P, KN, N], f32r)
        ln_w = sb("ln_w", [P, N])
        gain = sb("gain", [P, N])
        shift = sb("shift", [P, N])
        shift_h = sb("shift_h", [P, N])
        lnb_col = sb("lnb_col", [P, KN])
        lnb_hi = sb("lnb_hi", [P, KN, P], f32r)
        lnb_lo = sb("lnb_lo", [P, KN, P], f32r)
        gates = sb("gates", [P, 2])
        tanh_g = sb("tanh_g", [P, 2])
        w_maxes = sb("w_maxes", [P, KN])
        w_max = sb("w_max", [P, 1])
        w_scale = sb("w_scale", [P, 1])
        ident = sb("ident", [P, P])
        table_in = sb("table_in", [P, T])
        neg_half = sb("neg_half", [P, T])

        ctx_sb = sb("ctx_sb", [P, B, KC, L])
        ctx_hi = sb("ctx_hi", [P, B - WHOLE, KC, L], f32r)
        ctx_lo = sb("ctx_lo", [P, B - WHOLE, KC, L], f32r)
        x_sb = sb("x_sb", [P, T, N])
        xt_raw = sb("xt_raw", [P, T, KN, P])
        xt_hi = sb("xt_hi", [P, T, KN, P], f32r)
        xt_lo = sb("xt_lo", [P, T, KN, P], f32r)

        q_hi = sb("q_hi", [P, L], f32r)
        q_lo = sb("q_lo", [P, L], f32r)
        q_hi_later = sb("q_hi_later", [P, B, L], f32r)
        q_lo_later = sb("q_lo_later", [P, B, L], f32r)
        k_hi = sb("k_hi", [P, B, L], f32r)
        k_lo = sb("k_lo", [P, B, L], f32r)
        neg_max = sb("neg_max", [P, T])
        row_sum = sb("row_sum", [P, T])
        row_inv = sb("row_inv", [P, T])
        prob = sb("prob", [P, T, L])
        pt_hi = sb("pt_hi", [P, KN, L], f32r)
        pt_lo = sb("pt_lo", [P, KN, L], f32r)

        st1 = sb("st1", [P, T, 6])
        mv1 = sb("mv1", [P, T, 2])
        unread = sb("unread", [P, 2, N])
        neg_mean1 = sb("neg_mean1", [P, T])
        sq_sum1 = sb("sq_sum1", [P, T])
        var1 = sb("var1", [P, T])
        rstd1 = sb("rstd1", [P, T])
        y_scale = sb("y_scale", [P, T])
        y_bias = sb("y_bias", [P, T])
        st2 = sb("st2", [P, T, 6])
        mv2 = sb("mv2", [P, T, 2])
        var2 = sb("var2", [P, T])
        rstd2 = sb("rstd2", [P, T])

        x1 = sb("x1", [P, T, N])
        zw = sb("zw", [P, T, N])
        zt_hi = sb("zt_hi", [P, 2, KN, P], f32r)
        zt_lo = sb("zt_lo", [P, 2, KN, P], f32r)
        ffn = sb("ffn", [P, 3, N])

        ps_score = [pb(f"ps_score{i}", [P, L]) for i in range(2)]
        ps_turn = [pb(f"ps_turn{i}", [P, L]) for i in range(2)]
        ps_y = [pb(f"ps_y{i}", [P, L]) for i in range(2)]
        ps_ffn = [pb(f"ps_ffn{i}", [P, N]) for i in range(2)]

        wq_in = sem("wq_in")
        wk_in = sem("wk_in")
        ctx_in = [[sem(f"ctx_in{b}_{k}") for k in range(KC)] for b in range(B)]
        bias_in = sem("bias_in")
        gates_in = sem("gates_in")
        w_in = [sem(f"w_in{k}") for k in range(KN)]
        rows_in = sem("rows_in")
        table_done = sem("table_done")
        x_in = [sem(f"x_in{t}") for t in range(T)]
        xt_in = [sem(f"xt_in{t}") for t in range(T)]
        out_stored = [sem(f"out_stored{t}") for t in range(T)]
        ident_done = sem("ident_done")
        tanh_done = sem("tanh_done")
        sign_done = sem("sign_done")
        wmax_done = sem("wmax_done")
        scale_done = sem("scale_done")
        half_done = sem("half_done")
        lnb_done = sem("lnb_done")
        gain_done = sem("gain_done")
        shift_done = sem("shift_done")
        w_hi_done = sem("w_hi_done")
        w_lo_done = sem("w_lo_done")
        ctx_hi_done = sem("ctx_hi_done")
        ctx_lo_done = sem("ctx_lo_done")
        proj_ready = sem("proj_ready")
        proj_hi = sem("proj_hi")
        proj_lo = sem("proj_lo")
        q_moved = sem("q_moved")
        score_ready = sem("score_ready")
        pt_ready = sem("pt_ready")
        pt_hi_done = sem("pt_hi_done")
        pt_lo_done = sem("pt_lo_done")
        zt_ready = sem("zt_ready")
        zt_hi_done = sem("zt_hi_done")
        zt_lo_done = sem("zt_lo_done")
        y_ready = sem("y_ready")
        ffn_ready = sem("ffn_ready")
        ffn_evac = sem("ffn_evac")
        max_done = sem("max_done")
        exp_done = sem("exp_done")
        inv_done = sem("inv_done")
        prob_done = sem("prob_done")
        xt_hi_done = sem("xt_hi_done")
        xt_lo_done = sem("xt_lo_done")
        mean1_done = sem("mean1_done")
        square1_done = sem("square1_done")
        var1_done = sem("var1_done")
        scale1_done = sem("scale1_done")
        x_biased = sem("x_biased")
        later_zeroed = sem("later_zeroed")
        rstd1_done = sem("rstd1_done")
        ln1_done = sem("ln1_done")
        x1_done = sem("x1_done")
        stat1 = sem("stat1")
        stat2 = sem("stat2")
        rstd2_done = sem("rstd2_done")
        zw_done = sem("zw_done")
        x1b_done = sem("x1b_done")
        out_done = sem("out_done")
        last_out_done = sem("last_out_done")
        last_stored = sem("last_stored")

        STAT2 = 2 * T + 2

        block = es.enter_context(nc.Block())

        score_first = (ps_score[0], ps_score[1], ps_turn[0], ps_turn[1])
        prob_first = (ps_score[0], ps_score[1], ps_ffn[0], ps_y[1])
        prob_later = (ps_score[0], ps_score[1], ps_y[0], ps_y[1])
        proj_bank = (ps_ffn, ps_y, ps_ffn, ps_turn)

        halves = (slice(0, N // 2), slice(N // 2, N))
        half_bank = (ps_ffn[T % 2], ps_score[0])

        def prob_bank(b, t):
            return (prob_first if isinstance(b, int) else prob_later)[t]

        def score_bank(b, t):
            return score_first[t] if isinstance(b, int) else ps_score[t % 2]

        @block.sync
        def _(sp):
            def load_ctx(b):
                for k in range(KC):
                    sp.dma_start(ctx_sb[:, b, k, :], ctx_t[b, k * P:(k + 1) * P, :]).then_inc(ctx_in[b][k], 16)

            def load_xt(b, t):
                sp.dma_start(xt_raw[:, t, :, :], x_t[b, t, :, :, :]).then_inc(xt_in[t], 16)

            def load_x(b, t):
                sp.dma_start(x_sb[:, t, :], x[b, t * P:(t + 1) * P, :]).then_inc(x_in[t], 16)

            def store(b, t):
                sp.wait_ge(out_done, T * b + t + 1)
                sp.dma_start(out[b, t * P:(t + 1) * P, :], x1[:, t, :]).then_inc(out_stored[t], 16)

            for t in range(T):
                sp.sem_inc(out_stored[t], 16)
            sp.dma_start(wq_sb[:, :, :], wq_t.rearrange("(k p) d -> p k d", p=P)).then_inc(wq_in, 16)
            load_ctx(0)
            sp.dma_start(wk_sb[:, :, :], wk_t.rearrange("(k p) d -> p k d", p=P)).then_inc(wk_in, 16)
            load_ctx(1)
            for t in range(T):
                load_x(0, t)
            for b in range(2, B):
                load_ctx(b)
            for t in range(T):
                load_xt(0, t)
            for k in range(KN):
                sp.dma_start(w_raw[:, k, :], weight_t[k * P:(k + 1) * P, :]).then_inc(w_in[k], 16)
            for row, dst in ((ln_weight, ln_w), (gamma, gain), (beta, shift)):
                sp.dma_start(dst[:, :], row.rearrange("(a n) -> a n", a=1).broadcast_to([P, N]))\
                  .then_inc(rows_in, 16)

            def load_next(b, t):
                sp.wait_ge(x1_done, T * b + t + 1)
                load_x(b + 1, t)
                sp.wait_ge(xt_lo_done, T * b + t + 1)
                load_xt(b + 1, t)

            for t in range(T):
                load_next(0, t)
            store(0, 0)
            with sp.Fori(1, B - 1) as b:
                store(b - 1, 1)
                load_next(b, 0)
                store(b - 1, 2)
                load_next(b, 1)
                store(b - 1, T - 1)
                for t in range(2, T):
                    load_next(b, t)
                store(b, 0)
            for t in range(1, T):
                store(B - 2, t)
            for t in range(T - 2):
                store(B - 1, t)
            t = T - 1
            sp.wait_ge(last_out_done, 1)
            sp.dma_start(out[B - 1, (t - 1) * P:t * P, :], x1[:, t - 1, :]).then_inc(out_stored[t - 1], 16)
            for h, cols in enumerate(halves):
                sp.wait_ge(last_out_done, 2 + h)
                sp.dma_start(out[B - 1, t * P:(t + 1) * P, cols], x1[:, t, cols]).then_inc(last_stored, 16)
            sp.wait_ge(last_stored, 32)
            for t in range(T):
                sp.wait_ge(out_stored[t], 16 * (B + 1 if t < T - 1 else B))

        @block.tensor
        def _(pe):
            def project(b, j):
                if proj_bank[b] is ps_turn:
                    pe.wait_ge(exp_done, T)
                bank = proj_bank[b][j]
                if b < WHOLE:
                    for k in range(KC):
                        if j == 0:
                            pe.wait_ge(ctx_in[b][k], 16)
                        mm = pe.matmul(bank[:, :], (wq_sb, wk_sb)[j][:, k, :], ctx_sb[:, b, k, :],
                                       start=(k == 0), stop=(k == KC - 1))
                    mm.then_inc(proj_ready, 1)
                    return
                w_hi, w_lo = ((wq_hi, wq_lo), (wk_hi, wk_lo))[j]
                i = b - WHOLE
                pe.wait_ge(w_lo_done, 2)
                pe.wait_ge(ctx_hi_done, i + 1)
                for n, (lhs, rhs) in enumerate(((w_hi, ctx_hi), (w_lo, ctx_hi), (w_hi, ctx_lo))):
                    if n == 2:
                        pe.wait_ge(ctx_lo_done, i + 1)
                    for k in range(KC):
                        mm = pe.matmul(bank[:, :], lhs[:, k, :], rhs[:, i, k, :],
                                       start=(n == 0 and k == 0), stop=(n == 2 and k == KC - 1))
                mm.then_inc(proj_ready, 1)

            def scores(b, t):
                if isinstance(b, int):
                    if t == 0:
                        pe.wait_ge(proj_lo, 2)
                elif t == 0:
                    pe.wait_ge(q_moved, 2 * b)
                elif t >= 2:
                    pe.wait_ge(exp_done, T * b + t - 1)
                for i, (lhs, rhs) in enumerate(((q_hi, k_hi), (q_hi, k_lo), (q_lo, k_hi))):
                    mm = pe.matmul(score_bank(b, t)[:, :], lhs[:, t * P:(t + 1) * P], rhs[:, b, :],
                                   start=(i == 0), stop=(i == 2))
                mm.then_inc(score_ready, 1)

            def turn(bank, src, ready):
                for k in range(KN):
                    mm = pe.transpose(bank[:, k * P:(k + 1) * P], src[:, k * P:(k + 1) * P], ident[:, :])
                mm.then_inc(ready, 1)

            def turn_prob(b, t):
                pe.wait_ge(prob_done, T * b + t + 1)
                if isinstance(b, int):
                    if t >= 2:
                        pe.wait_ge(proj_lo, (5, 4)[t - 2])
                elif t < 2:
                    pe.wait_ge(exp_done, T * b + t + 3)
                else:
                    pe.wait_ge(x1_done, T * (b - 1) + t + 1)
                turn(prob_bank(b, t), prob[:, t, :], pt_ready)

            def turn_ffn(b, t):
                pe.wait_ge(zw_done, T * b + t + 1)
                turn(ps_turn[t % 2], zw[:, t, :], zt_ready)

            def attend(b, t):
                if t == 0:
                    pe.wait_ge(pt_hi_done, T * (b + 1))
                    if not isinstance(b, int):
                        pe.wait_ge(pt_lo_done, T * b + 3)
                pe.wait_ge(xt_lo_done, T * b + t + 1)
                if t >= 2:
                    pe.wait_ge(x1_done, T * b + t - 1)
                for i, (lhs, rhs) in enumerate(((xt_hi, pt_hi), (xt_lo, pt_hi), (xt_hi, pt_lo))):
                    if t == 0 and i == 2:
                        pe.wait_ge(pt_lo_done, T * (b + 1))
                    for k in range(KN):
                        mm = pe.matmul(ps_y[t % 2][:, :], lhs[:, t, k, :], rhs[:, k, :],
                                       start=(k == 0 and i == 0), stop=(k == KN - 1 and i == 2))
                mm.then_inc(y_ready, 1)

            def feed(b, t):
                pe.wait_ge(zt_hi_done, T * b + t + 1)
                pe.wait_ge(ffn_evac, T * b + max(t, 1))
                for i, lhs in enumerate((zt_hi, zt_lo)):
                    if i == 1:
                        pe.wait_ge(zt_lo_done, T * b + t + 1)
                    for k in range(KN):
                        mm = pe.matmul(ps_ffn[(t + 1) % 2][:, :], lhs[:, t % 2, k, :], w_sign[:, k, :],
                                       start=(k == 0 and i == 0), stop=(k == KN - 1 and i == 1))
                mm.then_inc(ffn_ready, 1)

            def back(b):
                scores(b + 1, 0)
                attend(b, 1)
                scores(b + 1, 1)
                turn_ffn(b, 0)
                attend(b, 2)
                turn_ffn(b, 1)
                scores(b + 1, 2)
                scores(b + 1, 3)
                feed(b, 0)
                attend(b, 3)
                turn_ffn(b, 2)
                turn_prob(b + 1, 0)
                turn_prob(b + 1, 1)
                turn_prob(b + 1, 2)
                feed(b, 1)
                turn_prob(b + 1, 3)
                feed(b, 2)
                turn_ffn(b, 3)
                attend(b + 1, 0)
                feed(b, 3)

            def last(b):
                attend(b, 1)
                attend(b, 2)
                turn_ffn(b, 0)
                attend(b, 3)
                turn_ffn(b, 1)
                feed(b, 0)
                turn_ffn(b, 2)
                feed(b, 1)
                turn_ffn(b, 3)
                feed(b, 2)
                t = T - 1
                pe.wait_ge(zt_lo_done, T * (b + 1))
                pe.wait_ge(ffn_evac, T * b + t)
                for h, cols in enumerate(halves):
                    for k in range(KN):
                        for i, lhs in enumerate((zt_hi, zt_lo)):
                            mm = pe.matmul(half_bank[h][:, cols], lhs[:, t % 2, k, :], w_sign[:, k, cols],
                                           start=(k == 0 and i == 0), stop=(k == KN - 1 and i == 1))
                    mm.then_inc(ffn_ready, 1)

            pe.wait_ge(later_zeroed, 2)
            for _ in range(WARM):
                pe.matmul(ps_score[0][:, :], q_hi_later[:, B - 1, :P], q_lo_later[:, B - 1, :],
                          start=True, stop=True)
            pe.wait_ge(wq_in, 16)
            project(0, 0)
            pe.wait_ge(wk_in, 16)
            project(0, 1)
            project(1, 0)
            for t in range(T):
                scores(0, t)
            project(1, 1)
            project(2, 0)
            project(2, 1)
            pe.wait_ge(ident_done, 2)
            turn_prob(0, 0)
            turn_prob(0, 1)
            project(3, 0)
            turn_prob(0, 2)
            turn_prob(0, 3)
            project(3, 1)
            attend(0, 0)
            pe.wait_ge(sign_done, 1)
            pe.wait_ge(lnb_done, 2)
            for k in range(KN):
                for i, lhs in enumerate((lnb_hi, lnb_lo)):
                    mm = pe.matmul(ps_ffn[0][:, :], lhs[:, k, :], w_sign[:, k, :],
                                   start=(k == 0 and i == 0), stop=(k == KN - 1 and i == 1))
            mm.then_inc(ffn_ready, 1)
            with pe.Fori(0, B - 1) as b:
                back(b)
            last(B - 1)

        @block.scalar
        def _(act):
            act.wait_ge(half_done, 1)
            nc.scalar.activation(table_in[:, :], neg_half[:, :], ACT.Tanh).then_inc(table_done, 1)
            act.wait_ge(table_done, 1)
            act.dma_start(bqk[:, 0:1], bq.rearrange("(p a) -> p a", a=1)).then_inc(bias_in, 16)
            act.dma_start(bqk[:, 1:2], bk.rearrange("(p a) -> p a", a=1)).then_inc(bias_in, 16)
            act.dma_start(gates[:, 0:1], g_xattn.rearrange("(a n) -> a n", a=1).broadcast_to([P, 1]))\
               .then_inc(gates_in, 16)
            act.dma_start(gates[:, 1:2], g_ffn.rearrange("(a n) -> a n", a=1).broadcast_to([P, 1]))\
               .then_inc(gates_in, 16)
            act.dma_start(lnb_col[:, :], ln_bias_t[:, :]).then_inc(gates_in, 16)

            def round_qk(b, j):
                dst = ((q_hi[:, :] if b == 0 else q_hi_later[:, b - 1, :]), k_hi[:, b, :])[j]
                act.wait_ge(proj_ready, 2 * b + j + 1)
                nc.scalar.activation(dst, proj_bank[b][j][:, :], ACT.Identity,
                                     bias=bqk[:, j:j + 1]).then_inc(proj_hi, 1)

            def round_ctx(b):
                for k in range(KC):
                    act.wait_ge(ctx_in[b][k], 16)
                nc.scalar.activation(ctx_hi[:, b - WHOLE, :, :], ctx_sb[:, b, :, :], ACT.Copy)\
                         .then_inc(ctx_hi_done, 1)

            def exps(b, t):
                act.wait_ge(max_done, T * b + t + 1)
                nc.scalar.activation(prob[:, t, :], score_bank(b, t)[:, :], ACT.Exp,
                                     bias=neg_max[:, t:t + 1], accum_out=row_sum[:, t:t + 1])\
                         .then_inc(exp_done, 1)

            def normalise(b, t):
                act.wait_ge(inv_done, T * b + t + 1)
                nc.scalar.activation(prob[:, t, :], prob[:, t, :], ACT.Copy,
                                     scale=row_inv[:, t:t + 1]).then_inc(prob_done, 1)

            def split_xt(b, t):
                act.wait_ge(xt_in[t], 16 * (b + 1))
                act.wait_ge(y_ready, T * (b - 1) + t + 1)
                nc.scalar.activation(xt_hi[:, t, :, :], xt_raw[:, t, :, :], ACT.Copy)\
                         .then_inc(xt_hi_done, 1)

            def stats_x(b, t):
                act.wait_ge(x_in[t], 16 * (b + 1))
                nc.scalar.activation(unread[:, 0, :], x_sb[:, t, :], ACT.Copy, scale=-1.0 / N,
                                     accum_out=neg_mean1[:, t:t + 1]).then_inc(mean1_done, 1)
                act.wait_ge(mean1_done, HALF * (b - 1) + t + 1)
                if t > 0:
                    act.wait_ge(square1_done, HALF * (b - 1) + t)
                nc.scalar.activation(unread[:, 1, :], x_sb[:, t, :], ACT.Square, bias=neg_mean1[:, t:t + 1],
                                     accum_out=sq_sum1[:, t:t + 1]).then_inc(square1_done, 1)

            def move_q(b):
                nc.scalar.activation(q_hi[:, :], q_hi_later[:, b, :], ACT.Copy).then_inc(q_moved, 1)
                nc.scalar.activation(q_lo[:, :], q_lo_later[:, b, :], ACT.Copy).then_inc(q_moved, 1)

            def bias_x(b):
                act.wait_ge(ln1_done, 2 * b + 1)
                for t in range(T):
                    nc.scalar.activation(x_sb[:, t, :], x_sb[:, t, :], ACT.Identity,
                                         bias=y_bias[:, t:t + 1]).then_inc(x_biased, 1)

            def turned_prob_hi(b, t):
                act.wait_ge(pt_ready, T * b + t + 1)
                nc.scalar.activation(pt_hi[:, :, t * P:(t + 1) * P],
                                     prob_bank(b, t)[:, :].rearrange("p (k m) -> p k m", k=KN), ACT.Copy)\
                         .then_inc(pt_hi_done, 1)

            def turned_ffn_hi(b, t):
                act.wait_ge(zt_ready, T * b + t + 1)
                nc.scalar.activation(zt_hi[:, t % 2, :, :],
                                     ps_turn[t % 2][:, :].rearrange("p (k m) -> p k m", k=KN), ACT.Copy)\
                         .then_inc(zt_hi_done, 1)

            def back(b):
                exps(b + 1, 0)
                stats_x(b + 1, 0)
                exps(b + 1, 1)
                normalise(b + 1, 0)
                turned_ffn_hi(b, 0)
                normalise(b + 1, 1)
                turned_ffn_hi(b, 1)
                exps(b + 1, 2)
                exps(b + 1, 3)
                move_q(b + 1)
                normalise(b + 1, 2)
                normalise(b + 1, 3)
                split_xt(b + 1, 0)
                turned_ffn_hi(b, 2)
                turned_prob_hi(b + 1, 0)
                turned_prob_hi(b + 1, 1)
                turned_prob_hi(b + 1, 2)
                stats_x(b + 1, 1)
                turned_prob_hi(b + 1, 3)
                split_xt(b + 1, 1)
                split_xt(b + 1, 2)
                turned_ffn_hi(b, 3)
                split_xt(b + 1, 3)
                bias_x(b + 1)

            for arrived, w, hi in ((wq_in, wq_sb, wq_hi), (wk_in, wk_sb, wk_hi)):
                act.wait_ge(arrived, 16)
                nc.scalar.activation(hi[:, :, :], w[:, :, :], ACT.Copy).then_inc(w_hi_done, 1)
            act.wait_ge(bias_in, 16 * 2)
            round_qk(0, 0)
            act.wait_ge(gates_in, 16 * 3)
            nc.scalar.activation(tanh_g[:, :], gates[:, :], ACT.Tanh).then_inc(tanh_done, 1)
            round_qk(0, 1)
            nc.scalar.activation(lnb_hi[:, :, :], lnb_col[:, :].unsqueeze(2).broadcast_to([P, KN, P]),
                                 ACT.Copy).then_inc(lnb_done, 1)
            round_qk(1, 0)
            round_ctx(WHOLE)
            exps(0, 0)
            exps(0, 1)
            exps(0, 2)
            exps(0, 3)
            round_qk(1, 1)
            normalise(0, 0)
            normalise(0, 1)
            round_qk(2, 0)
            normalise(0, 2)
            normalise(0, 3)
            round_qk(2, 1)
            for t in range(T):
                turned_prob_hi(0, t)
            round_qk(3, 0)
            round_qk(3, 1)
            for k in range(KN):
                act.wait_ge(w_in[k], 16)
            nc.scalar.activation(w_sign[:, :, :], w_raw[:, :, :], ACT.Sign).then_inc(sign_done, 1)
            bias_x(0)
            act.wait_ge(xt_hi_done, HALF)
            for t in range(HALF, T):
                act.wait_ge(xt_in[t], 16)
                nc.scalar.activation(xt_hi[:, t, :, :], xt_raw[:, t, :, :], ACT.Copy).then_inc(xt_hi_done, 1)
            act.wait_ge(rows_in, 48)
            nc.scalar.activation(shift[:, :], shift[:, :], ACT.Copy, scale=tanh_g[:, 1:2])\
                     .then_inc(shift_done, 1)
            act.wait_ge(ffn_ready, 1)
            nc.scalar.activation(shift_h[:, :], ps_ffn[0][:, :], ACT.Copy).then_inc(ffn_evac, 1)
            with act.Fori(0, B - 1) as b:
                back(b)
            for t in range(T):
                turned_ffn_hi(B - 1, t)

        @block.vector
        def _(dve):
            def row_max(b, t):
                dve.wait_ge(score_ready, T * b + t + 1)
                nc.vector.tensor_reduce(neg_max[:, t:t + 1], score_bank(b, t)[:, :], AX.X, ALU.max,
                                        negate=True).then_inc(max_done, 1)

            def invert(b, t):
                dve.wait_ge(exp_done, T * b + t + 1)
                nc.vector.reciprocal(row_inv[:, t:t + 1], row_sum[:, t:t + 1]).then_inc(inv_done, 1)

            def rest_qk(b, j):
                dst = ((q_lo[:, :] if b == 0 else q_lo_later[:, b - 1, :]), k_lo[:, b, :])[j]
                hi = ((q_hi[:, :] if b == 0 else q_hi_later[:, b - 1, :]), k_hi[:, b, :])[j]
                dve.wait_ge(proj_hi, 2 * b + j + 1)
                nc.vector.scalar_tensor_tensor(out=dst, in0=proj_bank[b][j][:, :], scalar=bqk[:, j:j + 1],
                                               in1=hi.bitcast(f32), op0=ALU.add, op1=ALU.subtract)\
                         .then_inc(proj_lo, 1)

            def round_ctx(b):
                for k in range(KC):
                    dve.wait_ge(ctx_in[b][k], 16)
                nc.vector.tensor_copy(ctx_hi[:, b - WHOLE, :, :], ctx_sb[:, b, :, :]).then_inc(ctx_hi_done, 1)

            def stats_x(b, tiles):
                for t in tiles:
                    dve.wait_ge(x_in[t], 16 * (b + 1))
                    nc.vector.bn_stats(st1[:, t, :], x_sb[:, t, :]).then_inc(stat1, 1)
                dve.drain()
                for t in tiles:
                    nc.vector.bn_aggr(mv1[:, t, :], st1[:, t, :]).then_inc(stat1, 1)

            def var_x(b):
                first = isinstance(b, int)
                cols = slice(0 if first else HALF, T)
                if not first:
                    dve.wait_ge(square1_done, HALF * b)
                    nc.vector.tensor_scalar(var1[:, :HALF], sq_sum1[:, :HALF], 1.0 / N, EPS,
                                            ALU.mult, ALU.add).then_inc(var1_done, 1)
                dve.wait_ge(stat1, 2 * T + 2 * HALF * b)
                nc.vector.tensor_scalar(var1[:, cols], mv1[:, cols, 1], EPS, None, ALU.add)\
                         .then_inc(var1_done, 1)

            def scale_x(b):
                first = isinstance(b, int)
                cols = slice(0 if first else HALF, T)
                dve.wait_ge(rstd1_done, b + 1)
                nc.vector.tensor_scalar(y_scale[:, :], rstd1[:, :], tanh_g[:, 0:1], None, ALU.mult)\
                         .then_inc(scale1_done, 1)
                dve.wait_ge(scale1_done, b + 1)
                if not first:
                    nc.vector.tensor_tensor(y_bias[:, :HALF], neg_mean1[:, :HALF], y_scale[:, :HALF],
                                            ALU.mult).then_inc(ln1_done, 1)
                nc.vector.scalar_tensor_tensor(out=y_bias[:, cols], in0=mv1[:, cols, 0], scalar=-1.0,
                                               in1=y_scale[:, cols], op0=ALU.mult, op1=ALU.mult)\
                         .then_inc(ln1_done, 1)

            def add_y(b, t):
                dve.wait_ge(out_stored[t], 16 * (b + 1))
                dve.wait_ge(x_biased, T * b + t + 1)
                dve.wait_ge(y_ready, T * b + t + 1)
                nc.vector.scalar_tensor_tensor(out=x1[:, t, :], in0=ps_y[t % 2][:, :],
                                               scalar=y_scale[:, t:t + 1], in1=x_sb[:, t, :],
                                               op0=ALU.mult, op1=ALU.add).then_inc(x1_done, 1)

            def mean_x1(b, t):
                dve.wait_ge(x1_done, T * b + t + 1)
                nc.vector.bn_stats(st2[:, t, :], x1[:, t, :]).then_inc(stat2, 1)
                dve.drain()
                nc.vector.bn_aggr(mv2[:, t, :], st2[:, t, :]).then_inc(stat2, 1)

            def centre(b, t):
                dve.wait_ge(stat2, STAT2 * b + 2 * t + 2 + t // HALF)
                nc.vector.scalar_tensor_tensor(out=zw[:, t, :], in0=x1[:, t, :], scalar=mv2[:, t, 0:1],
                                               in1=ln_w[:, :], op0=ALU.subtract, op1=ALU.mult)\
                         .then_inc(zw_done, 1)

            def var_both(b, half):
                cols = slice(half * HALF, (half + 1) * HALF)
                nc.vector.tensor_scalar(var2[:, cols], mv2[:, cols, 1], 1.0 + EPS, EPS * EPS,
                                        ALU.mult, ALU.add).then_inc(stat2, 1)

            def turned_prob_lo(b, t):
                dve.wait_ge(pt_hi_done, T * b + t + 1)
                cols = slice(t * P, (t + 1) * P)
                nc.vector.tensor_tensor(pt_lo[:, :, cols], prob_bank(b, t)[:, :].rearrange("p (k m) -> p k m", k=KN),
                                        pt_hi[:, :, cols].bitcast(f32), ALU.subtract).then_inc(pt_lo_done, 1)

            def turned_ffn_lo(b, t):
                dve.wait_ge(zt_hi_done, T * b + t + 1)
                nc.vector.tensor_tensor(zt_lo[:, t % 2, :, :],
                                        ps_turn[t % 2][:, :].rearrange("p (k m) -> p k m", k=KN),
                                        zt_hi[:, t % 2, :, :].bitcast(f32), ALU.subtract).then_inc(zt_lo_done, 1)

            def scale_ffn(b, t):
                dve.wait_ge(ffn_ready, 1 + T * b + t + 1)
                if t % HALF == 0:
                    dve.wait_ge(rstd2_done, 2 * b + t // HALF + 1)
                if t >= 2:
                    dve.wait_ge(out_done, T * b + t - 1)
                nc.vector.scalar_tensor_tensor(out=ffn[:, t % 2, :], in0=ps_ffn[(t + 1) % 2][:, :],
                                               scalar=rstd2[:, t:t + 1], in1=gain[:, :],
                                               op0=ALU.mult, op1=ALU.mult).then_inc(ffn_evac, 1)

            def back(b):
                row_max(b + 1, 0)
                mean_x1(b, 0)
                centre(b, 0)
                invert(b + 1, 0)
                add_y(b, 1)
                row_max(b + 1, 1)
                mean_x1(b, 1)
                centre(b, 1)
                invert(b + 1, 1)
                var_both(b, 0)
                turned_ffn_lo(b, 0)
                add_y(b, 2)
                row_max(b + 1, 2)
                turned_ffn_lo(b, 1)
                row_max(b + 1, 3)
                mean_x1(b, 2)
                invert(b + 1, 2)
                centre(b, 2)
                invert(b + 1, 3)
                stats_x(b + 1, (2,))
                add_y(b, 3)
                mean_x1(b, 3)
                scale_ffn(b, 0)
                turned_ffn_lo(b, 2)
                turned_prob_lo(b + 1, 0)
                centre(b, 3)
                var_both(b, 1)
                turned_prob_lo(b + 1, 1)
                turned_prob_lo(b + 1, 2)
                turned_prob_lo(b + 1, 3)
                stats_x(b + 1, (3,))
                var_x(b + 1)
                scale_ffn(b, 1)
                turned_ffn_lo(b, 3)
                scale_x(b + 1)
                scale_ffn(b, 2)
                add_y(b + 1, 0)
                scale_ffn(b, 3)

            def weight_max(k):
                dve.wait_ge(w_in[k], 16)
                nc.vector.tensor_reduce(w_maxes[:, k:k + 1], w_raw[:, k, :], AX.X, ALU.max,
                                        apply_absolute_value=True).then_inc(wmax_done, 1)

            def last(b):
                mean_x1(b, 0)
                centre(b, 0)
                add_y(b, 1)
                mean_x1(b, 1)
                centre(b, 1)
                var_both(b, 0)
                add_y(b, 2)
                turned_ffn_lo(b, 0)
                mean_x1(b, 2)
                centre(b, 2)
                add_y(b, 3)
                turned_ffn_lo(b, 1)
                mean_x1(b, 3)
                centre(b, 3)
                var_both(b, 1)
                scale_ffn(b, 0)
                turned_ffn_lo(b, 2)
                scale_ffn(b, 1)
                turned_ffn_lo(b, 3)
                scale_ffn(b, 2)
                dve.wait_ge(ffn_evac, 1 + T * b + 3)
                dve.wait_ge(x1b_done, T * b + 3)
                nc.vector.tensor_tensor(x1[:, 2, :], x1[:, 2, :], ffn[:, 0, :], ALU.add)\
                         .then_inc(last_out_done, 1)
                dve.wait_ge(x1b_done, T * b + 4)
                t = T - 1
                for h, cols in enumerate(halves):
                    dve.wait_ge(ffn_ready, 1 + T * b + t + 1 + h)
                    nc.vector.scalar_tensor_tensor(out=ffn[:, 2, cols], in0=half_bank[h][:, cols],
                                                   scalar=rstd2[:, t:t + 1], in1=gain[:, cols],
                                                   op0=ALU.mult, op1=ALU.mult).then_inc(ffn_evac, 1)
                    dve.wait_ge(ffn_evac, 1 + T * b + t + 1 + h)
                    nc.vector.tensor_tensor(x1[:, t, cols], x1[:, t, cols], ffn[:, 2, cols], ALU.add)\
                             .then_inc(last_out_done, 1)

            nc.vector.memset(q_lo_later[:, B - 1, :].bitcast(f32), 0.0).then_inc(later_zeroed, 1)
            for j, (w, hi, lo) in enumerate(((wq_sb, wq_hi, wq_lo), (wk_sb, wk_hi, wk_lo))):
                dve.wait_ge(w_hi_done, j + 1)
                nc.vector.tensor_tensor(lo[:, :, :], w[:, :, :], hi[:, :, :].bitcast(f32), ALU.subtract)\
                         .then_inc(w_lo_done, 1)
            dve.wait_ge(bias_in, 16 * 2)
            rest_qk(0, 0)
            stats_x(0, (0,))
            rest_qk(0, 1)
            for t in range(T):
                row_max(0, t)
            rest_qk(1, 0)
            for t in range(T):
                invert(0, t)
            for b in range(WHOLE + 1, B):
                round_ctx(b)
            rest_qk(1, 1)
            stats_x(0, range(1, T))
            var_x(0)
            rest_qk(2, 0)
            weight_max(0)
            rest_qk(2, 1)
            for t in range(T):
                turned_prob_lo(0, t)
            dve.wait_ge(tanh_done, 1)
            scale_x(0)
            rest_qk(3, 0)
            rest_qk(3, 1)
            dve.wait_ge(proj_lo, 2 * 2)
            dve.wait_ge(later_zeroed, 2)
            nc.vector.tensor_copy(q_hi[:, :], q_hi_later[:, 0, :]).then_inc(q_moved, 1)
            nc.vector.tensor_copy(q_lo[:, :], q_lo_later[:, 0, :]).then_inc(q_moved, 1)
            add_y(0, 0)
            weight_max(1)
            weight_max(2)
            weight_max(3)
            dve.wait_ge(wmax_done, KN)
            nc.vector.tensor_reduce(w_max[:, :], w_maxes[:, :], AX.X, ALU.max).then_inc(wmax_done, 1)
            dve.wait_ge(rows_in, 48)
            with dve.Fori(0, B - 1) as b:
                back(b)
            last(B - 1)

        @block.gpsimd
        def _(pool):
            def split_xt(b, t):
                pool.wait_ge(xt_hi_done, T * b + t + 1)
                nc.gpsimd.tensor_tensor(xt_lo[:, t, :, :], xt_raw[:, t, :, :],
                                        xt_hi[:, t, :, :].bitcast(f32), ALU.subtract).then_inc(xt_lo_done, 1)

            def add_shift(b, t):
                pool.wait_ge(zw_done, T * b + t + 1)
                nc.gpsimd.tensor_tensor(x1[:, t, :], x1[:, t, :], shift[:, :], ALU.add).then_inc(x1b_done, 1)

            def add_ffn(b, t):
                pool.wait_ge(ffn_evac, 1 + T * b + t + 1)
                pool.wait_ge(x1b_done, T * b + t + 1)
                nc.gpsimd.tensor_tensor(x1[:, t, :], x1[:, t, :], ffn[:, t % 2, :], ALU.add)\
                         .then_inc(out_done, 1)

            def power1(b):
                pool.wait_ge(var1_done, 2 * b + 1)
                nc.gpsimd.tensor_tensor(rstd1[:, :], var1[:, :], neg_half[:, :], ALU.pow)\
                         .then_inc(rstd1_done, 1)

            def power2(b, half):
                pool.wait_ge(stat2, STAT2 * b + (half + 1) * (2 * HALF + 1))
                cols = slice(half * HALF, (half + 1) * HALF)
                nc.gpsimd.tensor_tensor(rstd2[:, cols], var2[:, cols], neg_half[:, cols], ALU.pow)\
                         .then_inc(rstd2_done, 1)

            def back(b):
                add_shift(b, 0)
                add_shift(b, 1)
                power2(b, 0)
                split_xt(b + 1, 0)
                add_shift(b, 2)
                add_ffn(b, 0)
                add_shift(b, 3)
                power2(b, 1)
                split_xt(b + 1, 1)
                power1(b + 1)
                add_ffn(b, 1)
                split_xt(b + 1, 2)
                add_ffn(b, 2)
                split_xt(b + 1, 3)
                add_ffn(b, 3)

            def last(b):
                add_shift(b, 0)
                add_shift(b, 1)
                power2(b, 0)
                add_shift(b, 2)
                power2(b, 1)
                add_ffn(b, 0)
                add_ffn(b, 1)
                add_shift(b, 3)

            nc.gpsimd.memset(neg_half[:, :], -0.5).then_inc(half_done, 1)
            nc.gpsimd.memset(q_hi_later[:, B - 1, :].bitcast(f32), 0.0).then_inc(later_zeroed, 1)
            nc.gpsimd.memset(ident[:, :], 0.0).then_inc(ident_done, 1)
            pool.wait_ge(ident_done, 1)
            nc.gpsimd.affine_select(out=ident[:, :], in_=ident[:, :], compare_op=ALU.not_equal, fill=1.0,
                                    base=0, pattern=[[-1, P]], channel_multiplier=1).then_inc(ident_done, 1)
            pool.wait_ge(lnb_done, 1)
            nc.gpsimd.tensor_tensor(lnb_lo[:, :, :], lnb_col[:, :].unsqueeze(2).broadcast_to([P, KN, P]),
                                    lnb_hi[:, :, :].bitcast(f32), ALU.subtract).then_inc(lnb_done, 1)
            for b in range(WHOLE, B):
                pool.wait_ge(ctx_hi_done, b - WHOLE + 1)
                nc.gpsimd.tensor_tensor(ctx_lo[:, b - WHOLE, :, :], ctx_sb[:, b, :, :],
                                        ctx_hi[:, b - WHOLE, :, :].bitcast(f32), ALU.subtract)\
                         .then_inc(ctx_lo_done, 1)
            for t in range(HALF):
                pool.wait_ge(xt_in[t], 16)
                nc.gpsimd.tensor_copy(xt_hi[:, t, :, :], xt_raw[:, t, :, :]).then_inc(xt_hi_done, 1)
                split_xt(0, t)
                if t == 0:
                    pool.wait_ge(half_done, 1)
                    power1(0)
            pool.wait_ge(wmax_done, KN + 1)
            nc.gpsimd.partition_all_reduce(w_scale[:, :], w_max[:, :], P, bass.bass_isa.ReduceOp.max)\
                     .then_inc(scale_done, 1)
            for t in range(HALF, T):
                split_xt(0, t)
            pool.wait_ge(scale_done, 1)
            pool.wait_ge(tanh_done, 1)
            nc.gpsimd.tensor_tensor(w_scale[:, :], w_scale[:, :], tanh_g[:, 1:2], ALU.mult)\
                     .then_inc(scale_done, 1)
            pool.wait_ge(rows_in, 48)
            pool.wait_ge(scale_done, 2)
            nc.gpsimd.tensor_tensor(gain[:, :], gain[:, :], w_scale[:, 0:1].broadcast_to([P, N]), ALU.mult)\
                     .then_inc(gain_done, 1)
            pool.wait_ge(gain_done, 1)
            pool.wait_ge(ffn_evac, 1)
            nc.gpsimd.tensor_tensor(shift_h[:, :], shift_h[:, :], gain[:, :], ALU.mult).then_inc(shift_done, 1)
            pool.wait_ge(shift_done, 2)
            nc.gpsimd.tensor_tensor(shift[:, :], shift[:, :], shift_h[:, :], ALU.add).then_inc(shift_done, 1)
            pool.wait_ge(shift_done, 3)
            with pool.Fori(0, B - 1) as b:
                back(b)
            last(B - 1)


def kernel(x, ctx_1024, g_xattn, g_ffn, L0_xattn_Wq, L0_xattn_bq, L0_xattn_Wk, L0_xattn_bk,
           L0_ffn_weight, L0_ffn_gamma, L0_ffn_beta, L0_ffn_ln_weight, L0_ffn_ln_bias):
    import numpy as _np
    import concourse.bacc as _bacc
    from concourse import mybir as _mybir
    from concourse.bass_utils import run_bass_kernel_spmd as _run

    x = _np.asarray(x)
    B, L, N = x.shape
    P = 128
    x_t = x.reshape(B, L // P, P, N // P, P).transpose(0, 1, 4, 3, 2)
    feeds = {
        "x": x,
        "x_t": x_t,
        "ctx_t": _np.asarray(ctx_1024).transpose(0, 2, 1),
        "g_xattn": g_xattn,
        "g_ffn": g_ffn,
        "wq_t": _np.asarray(L0_xattn_Wq).T,
        "bq": L0_xattn_bq,
        "wk_t": _np.asarray(L0_xattn_Wk).T,
        "bk": L0_xattn_bk,
        "weight_t": _np.asarray(L0_ffn_weight).T,
        "gamma": L0_ffn_gamma,
        "beta": L0_ffn_beta,
        "ln_weight": L0_ffn_ln_weight,
        "ln_bias_t": _np.asarray(L0_ffn_ln_bias).reshape(N // P, P).T,
    }
    nc = _bacc.Bacc("TRN2", target_bir_lowering=False, num_devices=1)
    arrays, args = {}, []
    for name, a in feeds.items():
        a = _np.ascontiguousarray(a)
        arrays[f"in_{name}_dram"] = a
        args.append(nc.dram_tensor(f"in_{name}_dram", a.shape, _mybir.dt.from_np(a.dtype),
                                   kind="ExternalInput").ap())
    out = nc.dram_tensor("out_dram", (B, L, N), _mybir.dt.from_np(x.dtype), kind="ExternalOutput").ap()
    flamingo_block_kernel(nc, *args, out)
    r = _run(nc, [arrays], core_ids=[0])
    return r.results[0]["out_dram"]
```
